# Optimizing a Trainium2 kernel written in Bass

```python
import numpy as np
import jax
import jax.numpy as jnp

def _softmax(x, axis=-1):
    return jax.nn.softmax(x, axis=axis)

def _gelu(x):
    return jax.nn.gelu(x, approximate=True)

def _silu(x):
    return jax.nn.silu(x)

def _sigmoid(x):
    return jax.nn.sigmoid(x)

def _layernorm(x, axis=-1, eps=1e-05):
    m = jnp.mean(x, axis=axis, keepdims=True)
    v = jnp.var(x, axis=axis, keepdims=True)
    return (x - m) / jnp.sqrt(v + eps)

def _scatter_add(tgt, idx, src, axis=0):
    return tgt.at[idx].add(src)

def _segment_sum(src, seg, n):
    return jax.ops.segment_sum(src, seg, n)
kernel_name = 'mk_decoder_preln_d1_seqx_r8_4970b2'

def setup_inputs(seed: int=0):
    np.random.seed(seed)
    _w = jnp.asarray

    def _rec_inputs():
        import jax
        import jax.numpy as jnp
        _rk = jax.random.key(seed)
        x = 4.136e-05 + 0.9999 * jax.random.normal(jax.random.fold_in(_rk, 1), (4, 256, 256), jnp.float32)
        _lenS = 256 - jax.random.randint(jax.random.fold_in(_rk, 7), (4,), 0, max(1, 256 // 4) + 1, jnp.int32)
        _lenS2 = 256 - jax.random.randint(jax.random.fold_in(_rk, 8), (4,), 0, max(1, 256 // 4) + 1, jnp.int32)
        _ctx_1024P = jax.random.normal(jax.random.fold_in(_rk, 11), (4, 16, 128), jnp.float32)
        _ctx_1024c = jax.random.dirichlet(jax.random.fold_in(_rk, 511), 0.3 * jnp.ones((16,), jnp.float32), (4, 256))
        _ctx_1024t = jnp.einsum('bsk,bkd->bsd', _ctx_1024c, _ctx_1024P)
        _ctx_1024t = _ctx_1024t * jax.lax.rsqrt(jnp.mean(jnp.square(_ctx_1024t)) + 1e-12) * 0.953939
        ctx_1024 = -0.000292821 + 1.00034 * (_ctx_1024t + 0.3 * jax.random.normal(jax.random.fold_in(_rk, 611), (4, 256, 128), jnp.float32))
        return (x, ctx_1024)
    x, ctx_1024 = _rec_inputs()

    def _L0_attn_setup():
        import jax, jax.numpy as jnp
        import numpy as np
        B, S, HID = (1, 256, 256)
        H, KVH, HD = (32, 8, 64)
        THETA = 10000.0

        def _rotate_half(x):
            x1, x2 = jnp.split(x, 2, axis=-1)
            return jnp.concatenate([-x2, x1], axis=-1)

        def _rope_cos_sin(seq_len, head_dim, theta, dtype):
            inv_freq = 1.0 / theta ** (jnp.arange(0, head_dim, 2, dtype=jnp.float32) / head_dim)
            pos = jnp.arange(seq_len, dtype=jnp.float32)
            freqs = pos[:, None] * inv_freq[None, :]
            emb = jnp.concatenate([freqs, freqs], axis=-1)
            return (jnp.cos(emb).astype(dtype), jnp.sin(emb).astype(dtype))
        key = jax.random.key(seed)
        k0, k1, k2, k3, k4 = jax.random.split(key, 5)
        w = lambda k, shape: jax.random.normal(k, shape, dtype=jnp.float32) * 0.02
        return {'hidden_states': jax.random.normal(k0, (B, S, HID), dtype=jnp.float32), 'Wq': w(k1, (H * HD, HID)), 'Wk': w(k2, (KVH * HD, HID)), 'Wv': w(k3, (KVH * HD, HID)), 'Wo': w(k4, (HID, H * HD))}
    _L0_attn_all = _L0_attn_setup()
    _L0_attn_in = {k: v for k, v in _L0_attn_all.items() if k in ('Wq', 'Wk', 'Wv', 'Wo')}
    del _L0_attn_all

    def _L0_xattn_setup():
        import jax, jax.numpy as jnp
        import numpy as np
        import math
        B, L, DM = (2, 256, 128)
        DS, DC, EXP = (16, 4, 2)
        DI = EXP * DM
        DR = math.ceil(DM / 16)
        DT_MIN, DT_MAX, DT_FLOOR = (0.001, 0.1, 0.0001)

        def _ssm_forward(hidden_states, z, in_proj_w, conv_w, conv_b, x_proj_w, dt_proj_w, dt_proj_b, A_log, D):
            b = hidden_states.shape[0]
            x = jnp.einsum('ed,bld->bel', in_proj_w, hidden_states)
            xp = jnp.pad(x, ((0, 0), (0, 0), (DC - 1, 0)))
            xc = jax.lax.conv_general_dilated(xp, conv_w[:, None, :], window_strides=(1,), padding='VALID', dimension_numbers=('NCH', 'OIH', 'NCH'), feature_group_count=DI)
            u = jax.nn.silu(xc + conv_b[None, :, None])
            x_dbl = jnp.einsum('ke,bel->bkl', x_proj_w, u)
            dt_lo = x_dbl[:, :DR]
            Bm = x_dbl[:, DR:DR + DS]
            Cm = x_dbl[:, DR + DS:]
            delta = jax.nn.softplus(jnp.einsum('er,brl->bel', dt_proj_w, dt_lo) + dt_proj_b[None, :, None])
            A = -jnp.exp(A_log)

            def step(state, xs):
                d_t, B_t, C_t, u_t = xs
                dA = jnp.exp(d_t[..., None] * A)
                state = state * dA + (d_t * u_t)[..., None] * B_t[:, None, :]
                y_t = jnp.einsum('ben,bn->be', state, C_t)
                return (state, y_t)
            xs = (jnp.moveaxis(delta, -1, 0), jnp.moveaxis(Bm, -1, 0), jnp.moveaxis(Cm, -1, 0), jnp.moveaxis(u, -1, 0))
            state0 = jnp.zeros((b, DI, DS), delta.dtype)
            _, ys = jax.lax.scan(step, state0, xs)
            y = jnp.moveaxis(ys, 0, -1)
            y = y + D[None, :, None] * u
            y = y * jax.nn.silu(z)
            return jnp.swapaxes(y, 1, 2)
        key = jax.random.key(seed)
        ks = jax.random.split(key, 8)
        hidden_states = jax.random.normal(ks[0], (B, L, DM), jnp.float32)
        z = jax.random.normal(ks[1], (B, DI, L), jnp.float32)
        in_proj_w = jax.random.normal(ks[2], (DI, DM), jnp.float32) * DM ** (-0.5)
        conv_w = jax.random.normal(ks[3], (DI, DC), jnp.float32) * DC ** (-0.5)
        conv_b = jnp.zeros((DI,), jnp.float32)
        x_proj_w = jax.random.normal(ks[4], (DR + 2 * DS, DI), jnp.float32) * DI ** (-0.5)
        dt_std = DR ** (-0.5)
        dt_proj_w = jax.random.uniform(ks[5], (DI, DR), jnp.float32, -dt_std, dt_std)
        dt = jnp.exp(jax.random.uniform(ks[6], (DI,), jnp.float32) * (math.log(DT_MAX) - math.log(DT_MIN)) + math.log(DT_MIN))
        dt = jnp.clip(dt, DT_FLOOR)
        dt_proj_b = dt + jnp.log(-jnp.expm1(-dt))
        A_log = jnp.log(jnp.broadcast_to(jnp.arange(1, DS + 1, dtype=jnp.float32), (DI, DS)))
        D = jnp.ones((DI,), jnp.float32)
        return dict(hidden_states=hidden_states, z=z, in_proj_w=in_proj_w, conv_w=conv_w, conv_b=conv_b, x_proj_w=x_proj_w, dt_proj_w=dt_proj_w, dt_proj_b=dt_proj_b, A_log=A_log, D=D)
    _L0_xattn_all = _L0_xattn_setup()
    _L0_xattn_in = {k: v for k, v in _L0_xattn_all.items() if k in ('in_proj_w', 'conv_w', 'conv_b', 'x_proj_w', 'dt_proj_w', 'dt_proj_b', 'A_log', 'D')}
    del _L0_xattn_all

    def _L0_ffn_setup():
        import jax, jax.numpy as jnp
        import numpy as np
        DIM = 256
        HID = 704
        ZERO_POINT = 128.0

        def _qlinear(x, wq, scale):
            W = (wq.astype(jnp.float32) - ZERO_POINT) * scale[:, None]
            return jnp.einsum('bsd,hd->bsh', x, W)
        key = jax.random.key(seed)
        ks = jax.random.split(key, 7)
        B, S = (4, 256)
        sg = jax.random.uniform(ks[1], (HID,)) * (0.02 / np.sqrt(DIM)) + 0.0001
        su = jax.random.uniform(ks[3], (HID,)) * (0.02 / np.sqrt(DIM)) + 0.0001
        sd = jax.random.uniform(ks[5], (DIM,)) * (0.02 / np.sqrt(HID)) + 0.0001
        return {'x': jax.random.normal(ks[0], (B, S, DIM), dtype=jnp.float32), 'wq_gate': jax.random.randint(ks[2], (HID, DIM), 0, 32, dtype=jnp.int32), 's_gate': sg, 'wq_up': jax.random.randint(ks[4], (HID, DIM), 0, 32, dtype=jnp.int32), 's_up': su, 'wq_down': jax.random.randint(ks[6], (DIM, HID), 0, 32, dtype=jnp.int32), 's_down': sd}
    _L0_ffn_all = _L0_ffn_setup()
    _L0_ffn_in = {k: v for k, v in _L0_ffn_all.items() if k in ('wq_gate', 's_gate', 'wq_up', 's_up', 'wq_down', 's_down')}
    del _L0_ffn_all
    return {'x': x, 'ctx_1024': ctx_1024, 'L0_attn_Wq': _L0_attn_in['Wq'], 'L0_attn_Wk': _L0_attn_in['Wk'], 'L0_attn_Wv': _L0_attn_in['Wv'], 'L0_attn_Wo': _L0_attn_in['Wo'], 'L0_xattn_in_proj_w': _L0_xattn_in['in_proj_w'], 'L0_xattn_conv_w': _L0_xattn_in['conv_w'], 'L0_xattn_conv_b': _L0_xattn_in['conv_b'], 'L0_xattn_x_proj_w': _L0_xattn_in['x_proj_w'], 'L0_xattn_dt_proj_w': _L0_xattn_in['dt_proj_w'], 'L0_xattn_dt_proj_b': _L0_xattn_in['dt_proj_b'], 'L0_xattn_A_log': _L0_xattn_in['A_log'], 'L0_xattn_D': _L0_xattn_in['D'], 'L0_ffn_wq_gate': _L0_ffn_in['wq_gate'], 'L0_ffn_s_gate': _L0_ffn_in['s_gate'], 'L0_ffn_wq_up': _L0_ffn_in['wq_up'], 'L0_ffn_s_up': _L0_ffn_in['s_up'], 'L0_ffn_wq_down': _L0_ffn_in['wq_down'], 'L0_ffn_s_down': _L0_ffn_in['s_down']}

def reference(x, ctx_1024, L0_attn_Wq, L0_attn_Wk, L0_attn_Wv, L0_attn_Wo, L0_xattn_in_proj_w, L0_xattn_conv_w, L0_xattn_conv_b, L0_xattn_x_proj_w, L0_xattn_dt_proj_w, L0_xattn_dt_proj_b, L0_xattn_A_log, L0_xattn_D, L0_ffn_wq_gate, L0_ffn_s_gate, L0_ffn_wq_up, L0_ffn_s_up, L0_ffn_wq_down, L0_ffn_s_down):
    import jax
    import jax.numpy as jnp

    def _L0_attn_ref(hidden_states, Wq, Wk, Wv, Wo):
        import jax, jax.numpy as jnp
        import numpy as np
        B, S, HID = (1, 256, 256)
        H, KVH, HD = (32, 8, 64)
        THETA = 10000.0

        def _rotate_half(x):
            x1, x2 = jnp.split(x, 2, axis=-1)
            return jnp.concatenate([-x2, x1], axis=-1)

        def _rope_cos_sin(seq_len, head_dim, theta, dtype):
            inv_freq = 1.0 / theta ** (jnp.arange(0, head_dim, 2, dtype=jnp.float32) / head_dim)
            pos = jnp.arange(seq_len, dtype=jnp.float32)
            freqs = pos[:, None] * inv_freq[None, :]
            emb = jnp.concatenate([freqs, freqs], axis=-1)
            return (jnp.cos(emb).astype(dtype), jnp.sin(emb).astype(dtype))
        b, s, _ = hidden_states.shape
        dtype = hidden_states.dtype
        q = (hidden_states @ Wq.T).reshape(b, s, H, HD).transpose(0, 2, 1, 3)
        k = (hidden_states @ Wk.T).reshape(b, s, KVH, HD).transpose(0, 2, 1, 3)
        v = (hidden_states @ Wv.T).reshape(b, s, KVH, HD).transpose(0, 2, 1, 3)
        cos, sin = _rope_cos_sin(s, HD, THETA, dtype)
        apply_rope = lambda x: x * cos + _rotate_half(x) * sin
        q = apply_rope(q)
        k = apply_rope(k)
        groups = H // KVH
        k = jnp.repeat(k, groups, axis=1)
        v = jnp.repeat(v, groups, axis=1)
        scale = 1.0 / jnp.sqrt(jnp.asarray(HD, dtype=dtype))
        logits = jnp.einsum('bhqd,bhkd->bhqk', q, k) * scale
        causal = jnp.tril(jnp.ones((s, s), dtype=bool))
        logits = jnp.where(causal, logits, jnp.finfo(dtype).min)
        attn = jax.nn.softmax(logits, axis=-1)
        out = jnp.einsum('bhqk,bhkd->bhqd', attn, v)
        out = out.transpose(0, 2, 1, 3).reshape(b, s, H * HD)
        return out @ Wo.T

    def _L0_xattn_ref(hidden_states, z, in_proj_w, conv_w, conv_b, x_proj_w, dt_proj_w, dt_proj_b, A_log, D):
        import jax, jax.numpy as jnp
        import numpy as np
        import math
        B, L, DM = (2, 256, 128)
        DS, DC, EXP = (16, 4, 2)
        DI = EXP * DM
        DR = math.ceil(DM / 16)
        DT_MIN, DT_MAX, DT_FLOOR = (0.001, 0.1, 0.0001)

        def _ssm_forward(hidden_states, z, in_proj_w, conv_w, conv_b, x_proj_w, dt_proj_w, dt_proj_b, A_log, D):
            b = hidden_states.shape[0]
            x = jnp.einsum('ed,bld->bel', in_proj_w, hidden_states)
            xp = jnp.pad(x, ((0, 0), (0, 0), (DC - 1, 0)))
            xc = jax.lax.conv_general_dilated(xp, conv_w[:, None, :], window_strides=(1,), padding='VALID', dimension_numbers=('NCH', 'OIH', 'NCH'), feature_group_count=DI)
            u = jax.nn.silu(xc + conv_b[None, :, None])
            x_dbl = jnp.einsum('ke,bel->bkl', x_proj_w, u)
            dt_lo = x_dbl[:, :DR]
            Bm = x_dbl[:, DR:DR + DS]
            Cm = x_dbl[:, DR + DS:]
            delta = jax.nn.softplus(jnp.einsum('er,brl->bel', dt_proj_w, dt_lo) + dt_proj_b[None, :, None])
            A = -jnp.exp(A_log)

            def step(state, xs):
                d_t, B_t, C_t, u_t = xs
                dA = jnp.exp(d_t[..., None] * A)
                state = state * dA + (d_t * u_t)[..., None] * B_t[:, None, :]
                y_t = jnp.einsum('ben,bn->be', state, C_t)
                return (state, y_t)
            xs = (jnp.moveaxis(delta, -1, 0), jnp.moveaxis(Bm, -1, 0), jnp.moveaxis(Cm, -1, 0), jnp.moveaxis(u, -1, 0))
            state0 = jnp.zeros((b, DI, DS), delta.dtype)
            _, ys = jax.lax.scan(step, state0, xs)
            y = jnp.moveaxis(ys, 0, -1)
            y = y + D[None, :, None] * u
            y = y * jax.nn.silu(z)
            return jnp.swapaxes(y, 1, 2)
        return _ssm_forward(hidden_states, z, in_proj_w, conv_w, conv_b, x_proj_w, dt_proj_w, dt_proj_b, A_log, D)

    def _L0_ffn_ref(x, wq_gate, s_gate, wq_up, s_up, wq_down, s_down):
        import jax, jax.numpy as jnp
        import numpy as np
        DIM = 256
        HID = 704
        ZERO_POINT = 128.0

        def _qlinear(x, wq, scale):
            W = (wq.astype(jnp.float32) - ZERO_POINT) * scale[:, None]
            return jnp.einsum('bsd,hd->bsh', x, W)
        gate = _qlinear(x, wq_gate, s_gate)
        gate = jax.nn.silu(gate)
        up = _qlinear(x, wq_up, s_up)
        return _qlinear(gate * up, wq_down, s_down)
    x = x + _L0_attn_ref(_layernorm(x, axis=-1), L0_attn_Wq, L0_attn_Wk, L0_attn_Wv, L0_attn_Wo)
    x = x + _L0_xattn_ref(ctx_1024, _layernorm(x, axis=-1), L0_xattn_in_proj_w, L0_xattn_conv_w, L0_xattn_conv_b, L0_xattn_x_proj_w, L0_xattn_dt_proj_w, L0_xattn_dt_proj_b, L0_xattn_A_log, L0_xattn_D)
    x = x + _L0_ffn_ref(_layernorm(x, axis=-1), L0_ffn_wq_gate, L0_ffn_s_gate, L0_ffn_wq_up, L0_ffn_s_up, L0_ffn_wq_down, L0_ffn_s_down)
    return x

_drawn_inputs = setup_inputs


def setup_inputs(seed=0):
    import zlib

    import numpy as np

    out = dict(_drawn_inputs(seed))
    spreads = {'L0_xattn_conv_b': (0.0, 0.1), 'L0_xattn_D': (1.0, 0.2)}
    factors = {'L0_attn_Wq': 8.0,
     'L0_attn_Wk': 8.0,
     'L0_xattn_dt_proj_w': 6.223,
     'L0_ffn_s_gate': 8.0,
     'L0_ffn_s_up': 8.0,
     'L0_ffn_s_down': 8.0}
    for name, (base, spread) in spreads.items():
        noise = np.random.default_rng([zlib.crc32(name.encode()), seed]).standard_normal(out[name].shape)
        drawn = base * np.exp(spread * noise) if base else spread * noise
        out[name] = jnp.asarray(drawn.astype(out[name].dtype))
    for name, factor in factors.items():
        out[name] = (out[name] * factor).astype(out[name].dtype)
    return out
```

```python
from contextlib import ExitStack

import numpy as np

import concourse.bass as bass
from concourse import mybir

F32 = mybir.dt.float32
BF16 = mybir.dt.bfloat16
I32 = mybir.dt.int32
ALU = mybir.AluOpType
ACT = mybir.ActivationFunctionType
AX = mybir.AxisListType

P = 128
B, S, HID = 4, 256, 256
H, KVH, HD = 32, 8, 64
GRP = H // KVH
TB = S // P
KT = HID // P
UNITS = B * KVH
ROT = (GRP + 1) * HD
QKC = ROT + HD
GC = (GRP + 2) * HD
NS = 16
DM = 128
DI = 256
EB = DI // P
DC = 4
DR = 8
XR = DR + 2 * NS
L = B * S
HF = 704
HT = -(-HF // P)
HP = [min(P, HF - P * i) for i in range(HT)]
EPS = 1e-5
ZERO_POINT = 128.0
MASKED = -3.0e38
NPAR = DC + 3 + NS


def decoder_layer(nc, x, ctx_t, wqkv_t, wo_t, cos_t, sin_t, inproj_t, ssm_par, xproj_t, dtproj_t,
                  wgate_t, wup_t, wdown_t, s_gate, s_up, s_down, bc_scratch, out):
    ctx = ExitStack()
    with ctx:
        def sb(name, shape, dt=F32):
            return ctx.enter_context(nc.sbuf_tensor(name, shape, dt))

        def sem(name):
            return ctx.enter_context(nc.semaphore(name))

        wqkv = sb("wqkv", [P, KT, KVH, GC])
        wo = sb("wo", [P, H // 2, HID])
        wgu_i = sb("wgu_i", [P, 2, KT, HF], I32)
        wgu = wgu_i[:].bitcast(F32)
        wdn_i = sb("wdn_i", [P, HT, HID], I32)
        wdn = wdn_i[:].bitcast(F32)
        sgu = sb("sgu", [P, 2, HT])
        sdn = sb("sdn", [P, HID])
        cos_s = sb("cos_s", [P, TB, ROT])
        sin_s = sb("sin_s", [P, TB, ROT])
        xs = sb("xs", [P, B * TB, HID])
        x1 = sb("x1", [P, B * TB, HID])
        xt_all = sb("xt_all", [P, KT, L])
        xt = sb("xt", [P, KT, S])
        stats = sb("stats", [P, B * TB, 6])
        mv = sb("mv", [P, B * TB, 2])
        rstd = sb("rstd", [P, B * TB])
        mv1 = sb("mv1", [P, B * TB, 2])
        rstd1 = sb("rstd1", [P, B * TB])
        nmr1 = sb("nmr1", [P, B * TB])
        mv2 = sb("mv2", [P, TB, 2])
        rstd2 = sb("rstd2", [P, TB])
        half = sb("half", [P, B * TB])
        eps = sb("eps", [P, TB])
        ident = sb("ident", [P, P])
        ident_b = sb("ident_b", [P, P], BF16)
        mask0 = sb("mask0", [P, GRP * P], BF16)
        mask1 = sb("mask1", [P, 2 * S], BF16)
        ropec = sb("ropec", [P, TB, ROT])
        ropes = sb("ropes", [P, TB, ROT])
        qkn = sb("qkn", [P, 2, TB, QKC])
        qkt = sb("qkt", [P, 2, 3, S])
        vv = sb("vv", [P, 4, TB, HD])
        nmax = sb("nmax", [P, 2, 2 * GRP])
        rsum = sb("rsum", [P, 2, 2 * GRP])
        rinv = sb("rinv", [P, 2, 2 * GRP])
        prob0 = sb("prob0", [P, 2, GRP, P])
        prob1 = sb("prob1", [P, 2, GRP, S])
        pt = sb("pt", [P, 3, 4 * P])
        attn_t = sb("attn_t", [P, H // 2, S])
        par = sb("par", [P, EB, NPAR])
        a_neg = sb("a_neg", [P, EB, NS])
        a_exp = sb("a_exp", [P, EB, NS])
        inproj = sb("inproj", [P, DI])
        xproj = sb("xproj", [P, EB, XR])
        dtproj = sb("dtproj", [DR, DI])
        delta = sb("delta", [P, EB, L])
        du = sb("du", [P, EB, L])
        y = sb("y", [P, EB, L])
        decay = sb("decay", [P, 2, L])
        state = sb("state", [P, 2, L])
        bc = sb("bc", [P, 2, 2, L])
        ctxs = bc[:, 0, 0, :]
        u_s = bc[:, 1, :, :]
        conv_in = attn_t[:].rearrange("p a s -> p (a s)")[:, 0:EB * B * (S + DC - 1)].rearrange(
            "p (e b s) -> p e b s", e=EB, b=B)
        xdbl = attn_t[:].rearrange("p a s -> p (a s)")[0:XR, 3 * L:4 * L]
        flat_a = attn_t[:].rearrange("p a s -> p (a s)")
        sz = flat_a[:, 0:TB * HID].rearrange("p (t n) -> p t n", t=TB)
        gz = flat_a[:, TB * HID:2 * TB * HID].rearrange("p (t n) -> p t n", t=TB)
        xh2 = flat_a[:, 2 * TB * HID:3 * TB * HID].rearrange("p (t n) -> p t n", t=TB)
        xh2_t = flat_a[:, 3 * TB * HID:4 * TB * HID].rearrange("p (k n) -> p k n", k=KT)
        gate = ropec[:].rearrange("p t n -> p (t n)")[:, 0:2 * S].rearrange("p (r s) -> p r s", r=2)
        hid_t = prob1[:].rearrange("p a b s -> p (a b s)")[:, 0:HT * S].rearrange(
            "p (h s) -> p h s", h=HT)

        ps_s = ctx.enter_context(nc.psum_tensor("ps_s", [P, 3, 512], F32))
        ps_r = ctx.enter_context(nc.psum_tensor("ps_r", [P, 2, 512], F32))
        ps_p = ctx.enter_context(nc.psum_tensor("ps_p", [P, 2, 512], F32))
        ps_o = ctx.enter_context(nc.psum_tensor("ps_o", [P, 512], F32))

        x_in, ssm_in, wqkv_in, tab_in, wo_in, ffn_in = (
            sem(n) for n in ("x_in", "ssm_in", "wqkv_in", "tab_in", "wo_in", "ffn_in"))
        bc_out, bc_in0, bc_in1, out_done = (sem(n) for n in ("bc_out", "bc_in0", "bc_in1", "out_done"))
        bc_in = [bc_in0, bc_in1]
        consts = sem("consts")
        ln_stat, ln_rstd, ln_x = sem("ln_stat"), sem("ln_rstd"), sem("ln_x")
        xt_ps, xt_sb, xt_ready = sem("xt_ps"), sem("xt_sb"), sem("xt_ready")
        v_chain, p_chain = sem("v_chain"), sem("p_chain")
        inp_ps, inp_sb, conv_done, u_done = sem("inp_ps"), sem("inp_sb"), sem("conv_done"), sem("u_done")
        xdbl_ps, xdbl_sb, dt_ps, dt_v = sem("xdbl_ps"), sem("xdbl_sb"), sem("dt_ps"), sem("dt_v")
        sp_e, sp_w, sp_l, a_done = sem("sp_e"), sem("sp_w"), sem("sp_l"), sem("a_done")
        ssm_ready = sem("ssm_ready")
        proj_done = sem("proj_done")
        qkt_done = sem("qkt_done")
        score_done = sem("score_done")
        even_done = sem("even_done")
        pt_done = sem("pt_done")
        pv_done = sem("pv_done")
        wo_done = sem("wo_done")
        rope_mul = sem("rope_mul")
        v_copied = sem("v_copied")
        nmax_done = sem("nmax_done")
        rinv_done = sem("rinv_done")
        pt_dve = sem("pt_dve")
        pt_act = sem("pt_act")
        qkt_copied = sem("qkt_copied")
        exp_done = sem("exp_done")
        attn_copied = sem("attn_copied")
        rope_add = sem("rope_add")
        norm_done = sem("norm_done")
        decay_done = sem("decay_done")
        decay_free = sem("decay_free")
        drive_done = sem("drive_done")
        hc_done = sem("hc_done")
        state_free = sem("state_free")
        x1_done = sem("x1_done")
        st1_done = sem("st1_done")
        r1_done = sem("r1_done")
        sz_done, gz_done = sem("sz_done"), sem("gz_done")
        gt_ps, x2_done, st2_done, r2_done = sem("gt_ps"), sem("x2_done"), sem("st2_done"), sem("r2_done")
        xh2_done, x2t_ps, x2t_sb = sem("xh2_done"), sem("x2t_ps"), sem("x2t_sb")
        bn2_done = sem("bn2_done")
        gu_ps, gate_done, hid_done = sem("gu_ps"), sem("gate_done"), sem("hid_done")
        dn_ps, res_done = sem("dn_ps"), sem("res_done")
        wq_done = sem("wq_done")

        LAST = B - 1
        mulof = lambda v, k: k * v

        block = ctx.enter_context(nc.Block())

        @block.sync
        def _(sp):
            sp.dma_start(xs[:], x.rearrange("(t p) n -> p t n", p=P)).then_inc(x_in, 16)
            sp.dma_start(ctxs, ctx_t).then_inc(ssm_in, 16)
            sp.dma_start(inproj[:], inproj_t).then_inc(ssm_in, 16)
            sp.dma_start(par[:], ssm_par.rearrange("(e p) n -> p e n", p=P)).then_inc(ssm_in, 16)
            sp.dma_start(xproj[:], xproj_t.rearrange("(e p) n -> p e n", p=P)).then_inc(ssm_in, 16)
            sp.dma_start(dtproj[:], dtproj_t).then_inc(ssm_in, 16)
            sp.dma_start(wqkv[:], wqkv_t.rearrange("(k p) g n -> p k g n", p=P)).then_inc(wqkv_in, 16)
            sp.dma_start(cos_s[:], cos_t.rearrange("(t p) n -> p t n", p=P)).then_inc(tab_in, 16)
            sp.dma_start(sin_s[:], sin_t.rearrange("(t p) n -> p t n", p=P)).then_inc(tab_in, 16)
            sp.wait_ge(xdbl_sb, 2)
            sp.dma_start(bc_scratch, xdbl[DR:XR, :]).then_inc(bc_out, 16)
            sp.wait_ge(bc_out, 16)

            def load_bc(n):
                for c in range(2):
                    sp.dma_start(bc[:, n, c, :], bc_scratch[c * NS + n:c * NS + n + 1, :].to_broadcast([P, L])
                                 ).then_inc(bc_in[n], 16)

            load_bc(0)
            sp.dma_start(wo[:], wo_t.rearrange("(k p) n -> p k n", p=P)).then_inc(wo_in, 16)
            for i, w in enumerate((wgate_t, wup_t)):
                sp.dma_start(wgu_i[:, i, :, :], w.rearrange("(k p) n -> p k n", p=P)).then_inc(ffn_in, 16)
            full = P * (HT - 1)
            sp.dma_start(wdn_i[:, 0:HT - 1, :], wdown_t[0:full, :].rearrange("(k p) n -> p k n", p=P)
                         ).then_inc(ffn_in, 16)
            sp.dma_start(wdn_i[0:HP[-1], HT - 1, :], wdown_t[full:HF, :]).then_inc(ffn_in, 16)
            for i, s in enumerate((s_gate, s_up)):
                with nc.allow_non_contiguous_dma(reason="704 scales, once"):
                    sp.dma_start(sgu[:, i, 0:HT - 1], s[0:full].rearrange("(k p) -> p k", p=P)
                                 ).then_inc(ffn_in, 16)
                    sp.dma_start(sgu[0:HP[-1], i, HT - 1:HT], s[full:HF].rearrange("(p k) -> p k", k=1)
                                 ).then_inc(ffn_in, 16)
            sp.dma_start(sdn[:], s_down.rearrange("(a n) -> a n", a=1).to_broadcast([P, HID])
                         ).then_inc(ffn_in, 16)
            sp.wait_ge(ssm_ready, 5)
            load_bc(1)
            with sp.Fori(0, NS // 2 - 1) as j:
                for k in range(2):
                    sp.wait_ge(hc_done, j * 4 + 2 * k + 2)
                    for c in range(2):
                        sp.dma_start(bc[:, k, c, :],
                                     bc_scratch[bass.ds(j * 2 + (c * NS + k + 2), 1), :].to_broadcast([P, L])
                                     ).then_inc(bc_in[k], 16)
            with sp.Fori(0, B) as b:
                sp.wait_ge(res_done, b + 1)
                sp.dma_start(out[bass.ds(b, 1), :, :].rearrange("b (t p) n -> p (b t) n", p=P),
                             x1[:, bass.ds(b * TB, TB), :]).then_inc(out_done, 16)
            sp.wait_ge(out_done, 16 * B)

        @block.gpsimd
        def _(pool):
            pool.sem_inc(norm_done, 1)
            nc.gpsimd.memset(half[:], -0.5).then_inc(consts, 1)
            nc.gpsimd.memset(eps[:], EPS).then_inc(consts, 1)
            nc.gpsimd.memset(ident[:], 0.0).then_inc(consts, 1)
            nc.gpsimd.memset(ident_b[:], 0.0).then_inc(consts, 1)
            nc.gpsimd.memset(mask0[:], 0.0).then_inc(consts, 1)
            nc.gpsimd.memset(mask1[:], 0.0).then_inc(consts, 1)
            nc.gpsimd.memset(conv_in[:, :, :, 0:DC - 1], 0.0).then_inc(consts, 1)
            pool.wait_ge(consts, 7)
            for m in (ident, ident_b):
                nc.gpsimd.affine_select(out=m[:], in_=m[:], compare_op=ALU.not_equal, fill=1.0, base=0,
                                        pattern=[[-1, P]], channel_multiplier=1).then_inc(consts, 1)
            m0 = mask0[:].rearrange("p (h k) -> p h k", h=GRP)
            m1 = mask1[:].rearrange("p (h t k) -> p h t k", h=2, t=TB)[:, :, 1, :]
            nc.gpsimd.affine_select(out=m0, in_=m0, compare_op=ALU.is_ge, fill=MASKED, base=0,
                                    pattern=[[0, GRP], [-1, P]], channel_multiplier=1).then_inc(consts, 1)
            nc.gpsimd.affine_select(out=m1, in_=m1, compare_op=ALU.is_ge,
                                    fill=MASKED, base=0, pattern=[[0, 2], [-1, P]],
                                    channel_multiplier=1).then_inc(consts, 1)
            pool.wait_ge(ln_stat, B * TB)
            nc.gpsimd.tensor_scalar(rstd[:], mv[:, :, 1], EPS, 1.0, ALU.add, ALU.mult).then_inc(p_chain, 1)
            pool.wait_ge(p_chain, 1)
            nc.gpsimd.tensor_tensor(rstd[:], rstd[:], half[:], ALU.pow).then_inc(ln_rstd, 1)
            nc.gpsimd.memset(rsum[:], 0.0).then_inc(state_free, 1)
            nc.gpsimd.memset(rinv[:], 0.0).then_inc(state_free, 1)

            def add_rope(b, g):
                u = mulof(b, KVH) + g
                for t in range(TB):
                    pool.wait_ge(rope_mul, u * 4 + 2 * (t + 1))
                    if t == 0 and not (isinstance(b, int) and 8 * b + g < 2):
                        pool.wait_ge(qkt_done, u * 2 - 2)
                    o = qkn[:, g % 2, t, :]
                    nc.gpsimd.tensor_tensor(o[:, 0:ROT], ropec[:, t, :], ropes[:, t, :], ALU.add
                                            ).then_inc(rope_add, 1)
                    nc.gpsimd.tensor_tensor(o[:, ROT:QKC], ropec[:, t, ROT - HD:], ropes[:, t, ROT - HD:],
                                            ALU.add).then_inc(rope_add, 1)

            def normalise(b, g):
                u = mulof(b, KVH) + g
                pool.wait_ge(consts, 11)
                pool.wait_ge(rinv_done, u + 1)
                for h in range(GRP):
                    nc.gpsimd.tensor_scalar(prob0[:, g % 2, h, :], prob0[:, g % 2, h, :],
                                            rinv[:, g % 2, h:h + 1], 1.0, ALU.mult, ALU.mult
                                            ).then_inc(norm_done, 1)
                for h in range(GRP):
                    nc.gpsimd.tensor_scalar(prob1[:, g % 2, h, :], prob1[:, g % 2, h, :],
                                            rinv[:, g % 2, GRP + h:GRP + h + 1], 1.0, ALU.mult, ALU.mult
                                            ).then_inc(norm_done, 1)

            def add_y(b, g):
                u = mulof(b, KVH) + g
                pool.wait_ge(hc_done, u + 1)
                pool.wait_ge(state_free, u + 1)
                nc.gpsimd.tensor_tensor(y[:, g % 2, :], y[:, g % 2, :], state[:, g % 2, :], ALU.add
                                        ).then_inc(state_free, 1)

            add_rope(0, 0)
            add_rope(0, 1)
            normalise(0, 0)
            pool.wait_ge(ssm_ready, 5)

            def batch(b, last):
                for g in range(KVH):
                    if not (last and g + 2 >= KVH):
                        add_rope(b, g + 2)
                    if g > 0:
                        add_y(b, g - 1)
                    if not (last and g + 1 >= KVH):
                        normalise(b, g + 1)
                add_y(b, KVH - 1)

            with pool.Fori(0, LAST) as b:
                batch(b, False)
            batch(LAST, True)

            pool.wait_ge(st1_done, B * TB)
            nc.gpsimd.tensor_scalar(rstd1[:], mv1[:, :, 1], EPS, 1.0, ALU.add, ALU.mult).then_inc(p_chain, 1)
            pool.wait_ge(p_chain, 2)
            nc.gpsimd.tensor_tensor(rstd1[:], rstd1[:], half[:], ALU.pow).then_inc(r1_done, 1)

            def ffn_rstd(b):
                pool.wait_ge(st2_done, mulof(b, TB) + TB)
                nc.gpsimd.tensor_tensor(rstd2[:], mv2[:, :, 1], eps[:], ALU.add).then_inc(p_chain, 1)
                pool.wait_ge(p_chain, b + 3)
                nc.gpsimd.tensor_tensor(rstd2[:], rstd2[:], half[:, 0:TB], ALU.pow).then_inc(r2_done, 1)

            with pool.Fori(0, B) as b:
                ffn_rstd(b)

        @block.scalar
        def _(act):
            def copy_qkt(b, g):
                u = mulof(b, KVH) + g
                slot = g - 2
                for t in range(TB):
                    act.wait_ge(qkt_done, u * 2 + t + 1)
                    bank = (5 * slot + 3 + t) % 2
                    nc.scalar.activation(qkt[:, g % 2, :, t * P:(t + 1) * P],
                                         ps_r[:, bank, 0:3 * P].rearrange("p (k s) -> p k s", k=3), ACT.Copy
                                         ).then_inc(qkt_copied, 1)

            def exps(b, g, part):
                u = mulof(b, KVH) + g
                act.wait_ge(nmax_done, u * 3 + 3 - part)
                r = g % 2
                for k in range(GRP if part == 0 else 2):
                    if part == 0:
                        o, i, c = prob0[:, r, k, :], ps_s[:, 0, k * P:(k + 1) * P], k
                    else:
                        c = GRP + 2 * (part - 1) + k
                        o, i = prob1[:, r, c - GRP, :], ps_s[:, part, k * S:(k + 1) * S]
                    nc.scalar.activation(o, i, ACT.Exp, bias=nmax[:, r, c:c + 1],
                                         accum_out=rsum[:, r, c:c + 1]).then_inc(exp_done, 1)

            def copy_pt(b, g, fill):
                u = mulof(b, KVH) + g
                act.wait_ge(pt_done, u * 3 + fill + 1)
                nc.scalar.activation(pt[:, fill, :], ps_r[:, (5 * g + fill) % 2, :], ACT.Copy
                                     ).then_inc(pt_act, 1)

            def copy_attn(b, g):
                u = mulof(b, KVH) + g
                act.wait_ge(pv_done, u + 1)
                if g == 0 and not (isinstance(b, int) and b == 0):
                    act.wait_ge(wo_done, b + 1)
                nc.scalar.activation(attn_t[:, 2 * g:2 * g + 2, :],
                                     ps_o[:].rearrange("p (k s) -> p k s", k=2), ACT.Copy
                                     ).then_inc(attn_copied, 1)

            def decays(b, g):
                u = mulof(b, KVH) + g
                n = b * (KVH // 2) + g // 2
                act.wait_ge(decay_free, u + 1)
                nc.scalar.activation(
                    decay[:, g % 2, :].rearrange("p (b s) -> p b s", b=B)[:, :, 1:],
                    delta[:, g % 2, :].rearrange("p (b s) -> p b s", b=B)[:, :, 1:],
                    ACT.Exp, scale=a_neg[:, g % 2, bass.ds(n, 1)]).then_inc(decay_done, 1)

            act.sem_inc(pt_act, 1)
            act.sem_inc(attn_copied, 1)
            for i in range(B):
                act.wait_ge(xt_ps, i + 1)
                nc.scalar.activation(xt_all[:, :, i * S:(i + 1) * S],
                                     (ps_r[:, i % 2, :]).rearrange("p (k s) -> p k s", k=KT), ACT.Copy
                                     ).then_inc(xt_sb, 1)
            act.wait_ge(consts, 7)
            for i in range(2 * EB):
                e, h = divmod(i, 2)
                act.wait_ge(inp_ps, i + 1)
                src = ps_s[:, i, :] if i < 3 else ps_o[:]
                nc.scalar.activation(conv_in[:, e, 2 * h:2 * h + 2, DC - 1:],
                                     src.rearrange("p (b s) -> p b s", b=2), ACT.Copy).then_inc(inp_sb, 1)
            copy_qkt(0, 0)
            copy_qkt(0, 1)
            for e in range(EB):
                act.wait_ge(conv_done, DC * (e + 1))
                nc.scalar.activation(u_s[:, e, :], du[:, e, :], ACT.Silu).then_inc(u_done, 1)
            for i in range(2):
                act.wait_ge(xdbl_ps, i + 1)
                nc.scalar.activation(xdbl[:, i * 512:(i + 1) * 512], ps_p[0:XR, i, :], ACT.Copy
                                     ).then_inc(xdbl_sb, 1)
            for part in (2, 1, 0):
                exps(0, 0, part)
            nc.scalar.activation(a_exp[:], par[:, :, DC + 3:], ACT.Exp).then_inc(a_done, 1)
            for e in range(EB):
                act.wait_ge(dt_v, 2 * (e + 1))
                nc.scalar.activation(decay[:, e, :], delta[:, e, :], ACT.Abs).then_inc(sp_e, 1)
                act.wait_ge(sp_e, 2 * e + 1)
                nc.scalar.activation(decay[:, e, :], decay[:, e, :], ACT.Exp, scale=-1.0).then_inc(sp_e, 1)
            for e in range(EB):
                act.wait_ge(sp_w, e + 1)
                nc.scalar.activation(y[:, e, :], state[:, e, :], ACT.Ln).then_inc(sp_l, 1)

            act.wait_ge(ssm_ready, 5)
            act.wait_ge(bc_out, 16)
            decays(0, 0)

            def batch(b, last):
                for g in range(KVH):
                    copy_pt(b, g, 0)
                    nxt = not (last and g + 1 >= KVH)
                    if nxt:
                        exps(b, g + 1, 2)
                    copy_pt(b, g, 2)
                    if nxt:
                        exps(b, g + 1, 1)
                        exps(b, g + 1, 0)
                    if not (last and g + 2 >= KVH):
                        copy_qkt(b, g + 2)
                    copy_attn(b, g)
                    if not (last and g + 1 >= KVH):
                        decays(b, g + 1)

            with act.Fori(0, LAST) as b:
                batch(b, False)
            batch(LAST, True)

            act.wait_ge(r1_done, 2)
            act.wait_ge(ffn_in, 16 * 9)

            def silu_z(b):
                if not (isinstance(b, int) and b == 0):
                    act.wait_ge(gz_done, b)
                for t in range(TB):
                    nc.scalar.activation(sz[:, t, :], x1[:, bass.ds(b * TB + t, 1), :], ACT.Silu,
                                         bias=nmr1[:, bass.ds(b * TB + t, 1)],
                                         scale=rstd1[:, bass.ds(b * TB + t, 1)]).then_inc(sz_done, 1)

            def copy_x2t(b):
                act.wait_ge(x2t_ps, b + 1)
                nc.scalar.activation(xh2_t, ps_r[:, 1, :].rearrange("p (k s) -> p k s", k=KT),
                                     ACT.Copy).then_inc(x2t_sb, 1)

            def gates(b):
                for i in range(HT):
                    act.wait_ge(gu_ps, b * HT + i + 1)
                    if not (isinstance(b, int) and b == 0 and i < 2):
                        act.wait_ge(hid_done, b * HT + i - 1)
                    m = HP[i]
                    nc.scalar.activation(gate[0:m, i % 2, :], ps_s[0:m, i % 3, 0:S], ACT.Silu,
                                         scale=sgu[0:m, 0, i:i + 1]).then_inc(gate_done, 1)

            def ffn(b, last):
                if not last:
                    silu_z(b + 1)
                gates(b)
                if not last:
                    copy_x2t(b + 1)

            silu_z(0)
            copy_x2t(0)
            ffn(0, False)
            with act.Fori(1, LAST) as b:
                ffn(b, False)
            ffn(LAST, True)

        @block.vector
        def _(dve):
            chain = [0]

            def then(ins):
                chain[0] += 1
                ins.then_inc(v_chain, 1)
                dve.wait_ge(v_chain, chain[0])

            dve.sem_inc(pt_dve, 1)
            dve.sem_inc(x1_done, 1)
            dve.wait_ge(x_in, 16)
            for i in range(B * TB):
                nc.vector.bn_stats(stats[:, i, :], xs[:, i, :]).then_inc(v_chain, 1)
            chain[0] += B * TB
            dve.wait_ge(v_chain, chain[0])
            for i in range(B * TB):
                nc.vector.bn_aggr(mv[:, i, :], stats[:, i, :]).then_inc(ln_stat, 1)
            dve.wait_ge(ln_rstd, 1)
            dve.wait_ge(ln_stat, B * TB)
            for i in range(B * TB):
                nc.vector.tensor_scalar(x1[:, i, :], xs[:, i, :], mv[:, i, 0:1], rstd[:, i:i + 1],
                                        ALU.subtract, ALU.mult).then_inc(ln_x, 1)
            dve.wait_ge(xt_sb, 1)
            nc.vector.tensor_copy(xt[:], xt_all[:, :, 0:S]).then_inc(xt_ready, 1)

            def rope(b, g):
                u = mulof(b, KVH) + g
                for t in range(TB):
                    dve.wait_ge(proj_done, u * 2 + t + 1)
                    if not (isinstance(b, int) and 8 * b + g < 1):
                        dve.wait_ge(rope_add, u * 4 - 2 * (TB - 1 - t))
                    q = ps_p[:, t, 0:ROT]
                    nc.vector.tensor_tensor(ropec[:, t, :], q, cos_s[:, t, :], ALU.mult).then_inc(rope_mul, 1)
                    swapped = q.rearrange("p (h two d) -> p h two d", two=2, d=HD // 2)[:, :, ::-1, :]
                    nc.vector.tensor_tensor(
                        ropes[:, t, :].rearrange("p (h two d) -> p h two d", two=2, d=HD // 2), swapped,
                        sin_s[:, t, :].rearrange("p (h two d) -> p h two d", two=2, d=HD // 2),
                        ALU.mult).then_inc(rope_mul, 1)
                    nc.vector.tensor_copy(vv[:, g % 4, t, :], ps_p[:, t, ROT:GC]).then_inc(v_copied, 1)

            def negmax(b, g):
                u = mulof(b, KVH) + g
                for part in (2, 1, 0):
                    dve.wait_ge(score_done, u * 3 + 3 - part)
                    k, c = (GRP, 0) if part == 0 else (2, GRP + 2 * (part - 1))
                    nc.vector.tensor_reduce(nmax[:, g % 2, c:c + k],
                                            ps_s[:, part, :].rearrange("p (k s) -> p k s", k=k),
                                            AX.X, ALU.max, negate=True).then_inc(nmax_done, 1)

            def reciprocals(b, g):
                u = mulof(b, KVH) + g
                dve.wait_ge(exp_done, u * 8 + 8)
                if not (isinstance(b, int) and 8 * b + g < 2):
                    dve.wait_ge(norm_done, u * 8 - 7)
                nc.vector.reciprocal(rinv[:, g % 2, :], rsum[:, g % 2, :]).then_inc(rinv_done, 1)

            dve.wait_ge(tab_in, 32)
            rope(0, 0)
            rope(0, 1)

            dve.wait_ge(ssm_in, 16 * 5)
            for e in range(EB):
                dve.wait_ge(inp_sb, 2 * (e + 1))
                acc = du[:, e, :].rearrange("p (b s) -> p b s", b=B)
                nc.vector.tensor_scalar(acc, conv_in[:, e, :, 0:S], par[:, e, 0:1], par[:, e, DC:DC + 1],
                                        ALU.mult, ALU.add).then_inc(conv_done, 1)
                for j in range(1, DC):
                    dve.wait_ge(conv_done, DC * e + j)
                    nc.vector.scalar_tensor_tensor(acc, conv_in[:, e, :, j:j + S], par[:, e, j:j + 1], acc,
                                                   ALU.mult, ALU.add).then_inc(conv_done, 1)
            negmax(0, 0)
            for e in range(EB):
                for h in range(2):
                    dve.wait_ge(dt_ps, 2 * e + h + 1)
                    nc.vector.tensor_scalar(delta[:, e, h * 512:(h + 1) * 512], ps_r[:, h, :],
                                            par[:, e, DC + 1:DC + 2], None, ALU.add).then_inc(dt_v, 1)
            reciprocals(0, 0)
            for e in range(EB):
                dve.wait_ge(sp_e, 2 * (e + 1))
                nc.vector.tensor_scalar(state[:, e, :], decay[:, e, :], 1.0, None, ALU.add).then_inc(sp_w, 1)
            dve.wait_ge(a_done, 1)
            nc.vector.tensor_scalar(a_neg[:], a_exp[:], -1.0, None, ALU.mult).then_inc(ssm_ready, 1)
            for e in range(EB):
                dve.wait_ge(sp_w, e + 1)
                then(nc.vector.scalar_tensor_tensor(decay[:, e, :], state[:, e, :], 1.0, decay[:, e, :],
                                                    ALU.subtract, ALU.subtract))
                dve.wait_ge(sp_l, e + 1)
                then(nc.vector.tensor_tensor(y[:, e, :], y[:, e, :], decay[:, e, :], ALU.subtract))
                then(nc.vector.scalar_tensor_tensor(delta[:, e, :], delta[:, e, :], 0.0, y[:, e, :],
                                                    ALU.max, ALU.add))
                dve.wait_ge(u_done, e + 1)
                nc.vector.tensor_tensor(du[:, e, :], delta[:, e, :], u_s[:, e, :], ALU.mult
                                        ).then_inc(ssm_ready, 1)
                nc.vector.tensor_scalar(y[:, e, :], u_s[:, e, :], par[:, e, DC + 2:DC + 3], None, ALU.mult
                                        ).then_inc(ssm_ready, 1)
            for r in range(2):
                nc.vector.memset(decay[:, r, :].rearrange("p (b s) -> p b s", b=B)[:, :, 0:1], 0.0
                                 ).then_inc(decay_free, 1)
            dve.wait_ge(ssm_ready, 5)
            dve.wait_ge(decay_free, 2)
            dve.wait_ge(xt_sb, B)

            def drive(b, g):
                u = mulof(b, KVH) + g
                n = b * (KVH // 2) + g // 2
                r = (g // 2) % 2
                dve.wait_ge(bc_in[r], (b * 2 + g // 4 + 1) * 32)
                dve.wait_ge(state_free, u + 1)
                nc.vector.tensor_tensor(state[:, g % 2, :], du[:, g % 2, :], bc[:, r, 0, :], ALU.mult
                                        ).then_inc(drive_done, 1)

            def scan(b, g):
                u = mulof(b, KVH) + g
                dve.wait_ge(drive_done, u + 1)
                dve.wait_ge(decay_done, u + 1)
                nc.vector.tensor_tensor_scan(state[:, g % 2, :], decay[:, g % 2, :], state[:, g % 2, :], 0.0,
                                             ALU.mult, ALU.add).then_inc(decay_free, 1)

            def times_c(b, g):
                u = mulof(b, KVH) + g
                dve.wait_ge(decay_free, u + 3)
                nc.vector.tensor_tensor(state[:, g % 2, :], state[:, g % 2, :],
                                        bc[:, (g // 2) % 2, 1, :], ALU.mult).then_inc(hc_done, 1)

            def copy_pt(b, g):
                u = mulof(b, KVH) + g
                dve.wait_ge(pt_done, u * 3 + 2)
                nc.vector.tensor_copy(pt[:, 1, :], ps_r[:, (5 * g + 1) % 2, :]).then_inc(pt_dve, 1)

            def next_x(b):
                dve.wait_ge(proj_done, b * 16 + 16)
                nc.vector.tensor_copy(xt[:], xt_all[:, :, bass.ds((b + 1) * S, S)]).then_inc(xt_ready, 1)

            def add_attention(b):
                dve.wait_ge(wo_done, b + 2)
                nc.vector.tensor_tensor(x1[:, bass.ds(b * TB, TB), :],
                                        ps_o[:].rearrange("p (t n) -> p t n", t=TB),
                                        xs[:, bass.ds(b * TB, TB), :], ALU.add).then_inc(x1_done, 1)

            def dequantise():
                dve.wait_ge(ffn_in, 16 * 9)
                nc.vector.tensor_scalar(wgu, wgu_i[:], ZERO_POINT, None, ALU.subtract).then_inc(wq_done, 1)
                for i in range(HT):
                    m = HP[i]
                    nc.vector.scalar_tensor_tensor(wdn[0:m, i, :], wdn_i[0:m, i, :], ZERO_POINT,
                                                   sdn[0:m, :], ALU.subtract, ALU.mult).then_inc(wq_done, 1)

            def batch(b, last):
                for g in range(KVH):
                    if g == 5 and not last:
                        next_x(b)
                    if not (last and g + 2 >= KVH):
                        rope(b, g + 2)
                    if not (last and g + 1 >= KVH):
                        negmax(b, g + 1)
                    copy_pt(b, g)
                    drive(b, g)
                    scan(b, g)
                    if not (last and g + 1 >= KVH):
                        reciprocals(b, g + 1)
                    times_c(b, g)
                add_attention(b)

            with dve.Fori(0, LAST) as b:
                batch(b, False)
            batch(LAST, True)

            dve.wait_ge(x1_done, 1 + B)
            for i in range(B * TB):
                nc.vector.bn_stats(stats[:, i, :], x1[:, i, :]).then_inc(v_chain, 1)
            chain[0] += B * TB
            dve.wait_ge(v_chain, chain[0])
            for i in range(B * TB):
                nc.vector.bn_aggr(mv1[:, i, :], stats[:, i, :]).then_inc(st1_done, 1)
            dequantise()
            dve.wait_ge(r1_done, 1)
            nc.vector.scalar_tensor_tensor(nmr1[:], mv1[:, :, 0], -1.0, rstd1[:], ALU.mult, ALU.mult
                                           ).then_inc(r1_done, 1)
            dve.wait_ge(state_free, UNITS + 2)

            def gate_z(b):
                dve.wait_ge(sz_done, b * TB + TB)
                if not (isinstance(b, int) and b == 0):
                    dve.wait_ge(gt_ps, b)
                nc.vector.tensor_tensor(gz, y[:, :, bass.ds(b * S, S)], sz, ALU.mult).then_inc(gz_done, 1)

            def norm_x2(b):
                dve.wait_ge(gt_ps, b + 1)
                nc.vector.tensor_tensor(xs[:, bass.ds(b * TB, TB), :],
                                        ps_r[:, 0, :].rearrange("p (t n) -> p t n", t=TB),
                                        x1[:, bass.ds(b * TB, TB), :], ALU.add).then_inc(x2_done, 1)
                dve.wait_ge(x1_done, 1 + B)
                dve.wait_ge(x2_done, b + 1)
                for t in range(TB):
                    nc.vector.bn_stats(stats[:, t, :], xs[:, bass.ds(b * TB + t, 1), :].rearrange(
                        "p a n -> p (a n)")).then_inc(bn2_done, 1)
                dve.wait_ge(x1_done, 1 + B)
                dve.wait_ge(bn2_done, b * TB + TB)
                for t in range(TB):
                    nc.vector.bn_aggr(mv2[:, t, :], stats[:, t, :]).then_inc(st2_done, 1)
                dve.wait_ge(r2_done, b + 1)
                dve.wait_ge(st2_done, b * TB + TB)
                for t in range(TB):
                    nc.vector.tensor_scalar(xh2[:, t, :], xs[:, bass.ds(b * TB + t, 1), :], mv2[:, t, 0:1],
                                            rstd2[:, t:t + 1], ALU.subtract, ALU.mult).then_inc(xh2_done, 1)

            def hidden(b):
                for i in range(HT):
                    m = HP[i]
                    dve.wait_ge(gate_done, b * HT + i + 1)
                    if i == 0 and not (isinstance(b, int) and b == 0):
                        dve.wait_ge(dn_ps, b * TB)
                    nc.vector.scalar_tensor_tensor(hid_t[0:m, i, :], ps_s[0:m, i % 3, S:2 * S],
                                                   sgu[0:m, 1, i:i + 1], gate[0:m, i % 2, :],
                                                   ALU.mult, ALU.mult).then_inc(hid_done, 1)

            def result(b):
                dve.wait_ge(dn_ps, b * TB + TB)
                nc.vector.tensor_tensor(x1[:, bass.ds(b * TB, TB), :], ps_p[:, :, 0:HID],
                                        xs[:, bass.ds(b * TB, TB), :], ALU.add).then_inc(res_done, 1)

            def ffn(b, last):
                if not last:
                    gate_z(b + 1)
                hidden(b)
                if not last:
                    norm_x2(b + 1)
                result(b)

            gate_z(0)
            norm_x2(0)
            ffn(0, False)
            with dve.Fori(1, LAST) as b:
                ffn(b, False)
            ffn(LAST, True)

        @block.tensor
        def _(pe):
            pe.sem_inc(wo_done, 1)
            pe.wait_ge(consts, 11)

            def transpose_x(i):
                pe.wait_ge(ln_x, TB * (i + 1))
                if i >= 2:
                    pe.wait_ge(xt_sb, i - 1)
                for k in range(KT):
                    for t in range(TB):
                        last = nc.tensor.transpose(ps_r[:, i % 2, k * S + t * P:k * S + (t + 1) * P],
                                                   x1[:, i * TB + t, k * P:(k + 1) * P], ident[:])
                last.then_inc(xt_ps, 1)

            for i in range(B):
                transpose_x(i)

            def project(b, g):
                u = mulof(b, KVH) + g
                gg = g % KVH
                if gg == 0:
                    pe.wait_ge(xt_ready, b + 1 + g // KVH)
                for t in range(TB):
                    if not (isinstance(b, int) and 8 * b + g < 1):
                        pe.wait_ge(rope_mul, u * 4 - 2 * (TB - 1 - t))
                        pe.wait_ge(v_copied, u * 2 - (TB - 1 - t))
                    for k in range(KT):
                        last = nc.tensor.matmul(ps_p[:, t, 0:GC], xt[:, k, t * P:(t + 1) * P],
                                                wqkv[:, k, gg, :], start=(k == 0), stop=(k == KT - 1))
                    last.then_inc(proj_done, 1)

            def transpose_qk(b, g):
                u = mulof(b, KVH) + g
                slot = g - 2
                for t in range(TB):
                    pe.wait_ge(rope_add, u * 4 + 2 * (t + 1))
                    bank = (5 * slot + 3 + t) % 2
                    if t == 0:
                        if isinstance(b, int) and b == 0 and g == 0:
                            pe.wait_ge(xt_sb, B)
                        else:
                            pe.wait_ge(qkt_copied, u * 2)
                        if slot >= 0:
                            pe.wait_ge(pt_dve, u)
                    elif slot >= 0:
                        pe.wait_ge(pt_act, u * 2 - 1)
                    for k in range(3):
                        last = nc.tensor.transpose(ps_r[:, bank, k * P:(k + 1) * P],
                                                   qkn[:, g % 2, t, k * P:(k + 1) * P], ident[:])
                    last.then_inc(qkt_done, 1)

            def scores(b, g):
                u = mulof(b, KVH) + g
                r = g % 2
                pe.wait_ge(qkt_copied, u * 2 + 2)
                first = isinstance(b, int) and 8 * b + g < 1

                def dot(bank, col, h, t, keys, **kw):
                    lo = (h % 2) * HD
                    return nc.tensor.matmul(ps_s[:, bank, col:col + keys],
                                            qkt[lo:lo + HD, r, h // 2, t * P:(t + 1) * P],
                                            qkt[lo:lo + HD, r, 2, 0:keys], start=False, **kw)

                if first:
                    pe.wait_ge(inp_sb, 2 * EB)
                else:
                    pe.wait_ge(exp_done, u * 8)
                for bank, m in ((2, mask1), (0, mask0), (1, mask1)):
                    nc.tensor.matmul(ps_s[:, bank, :], ident_b[:], m[:], start=True, stop=False)
                dot(0, 0, 0, 0, P, stop=False)
                dot(2, 0, 1, 1, S, stop=False)
                dot(0, 2 * P, 2, 0, P, stop=False).then_inc(even_done, 1)
                dot(2, S, 3, 1, S, stop=True).then_inc(score_done, 1)
                dot(1, 0, 0, 1, S, stop=False)
                pe.wait_ge(even_done, u + 1)
                dot(0, P, 1, 0, P, stop=False)
                dot(1, S, 2, 1, S, stop=True).then_inc(score_done, 1)
                dot(0, 3 * P, 3, 0, P, stop=True).then_inc(score_done, 1)

            place = [0, 2, 1, 3]

            def transpose_p(b, g, qk_before):
                u = mulof(b, KVH) + g
                r = g % 2
                pe.wait_ge(norm_done, u * 8 + 9)
                for fill in range(3):
                    bank = (5 * g + fill) % 2
                    if fill == 2:
                        pe.wait_ge(pt_act, u * 2 + 2)
                    elif qk_before:
                        pe.wait_ge(qkt_copied, u * 2 + 3 + fill)
                    elif fill == 0:
                        pe.wait_ge(pt_dve, u + 1)
                    else:
                        pe.wait_ge(pt_act, u * 2 + 1)
                    for k in range(4):
                        if fill < 2:
                            h = 2 * fill + k // 2
                            src = prob0[:, r, h, :] if k % 2 == 0 else prob1[:, r, place[h], 0:P]
                        else:
                            src = prob1[:, r, place[k], P:S]
                        last = nc.tensor.transpose(ps_r[:, bank, k * P:(k + 1) * P], src, ident[:])
                    last.then_inc(pt_done, 1)

            def values(b, g):
                u = mulof(b, KVH) + g
                if not (isinstance(b, int) and 8 * b + g < 1):
                    pe.wait_ge(attn_copied, u + 1)
                    if g == 0:
                        pe.wait_ge(x1_done, b + 1)
                pe.wait_ge(v_copied, u * 2 + 2)
                pe.wait_ge(pt_act, u * 2 + 3)
                pe.wait_ge(pt_dve, u + 2)
                for pair in range(GRP // 2):
                    for part in range(2):
                        for odd in range(2):
                            o = ps_o[odd * HD:(odd + 1) * HD, :]
                            if part == 0:
                                last = nc.tensor.matmul(o[:, pair * S:(pair + 1) * S], vv[:, g % 4, 0, :],
                                                        pt[:, pair, odd * S:(odd + 1) * S], start=True, stop=False)
                            else:
                                h = 2 * pair + odd
                                last = nc.tensor.matmul(o[:, pair * S + P:(pair + 1) * S], vv[:, g % 4, 1, :],
                                                        pt[:, 2, h * P:(h + 1) * P], start=False, stop=True)
                last.then_inc(pv_done, 1)

            def out_project(b):
                pe.wait_ge(wo_in, 16)
                pe.wait_ge(attn_copied, b * 8 + 9)
                for t in range(TB):
                    for k in range(H // 2):
                        last = nc.tensor.matmul(ps_o[:, t * HID:(t + 1) * HID], attn_t[:, k, t * P:(t + 1) * P],
                                                wo[:, k, :], start=(k == 0), stop=(k == H // 2 - 1))
                last.then_inc(wo_done, 1)

            pe.wait_ge(wqkv_in, 16)
            project(0, 0)
            project(0, 1)
            pe.wait_ge(ssm_in, 16 * 5)
            for i in range(2 * EB):
                e, h = divmod(i, 2)
                dst = ps_s[:, i, :] if i < 3 else ps_o[:]
                nc.tensor.matmul(dst, inproj[:, e * P:(e + 1) * P], ctxs[:, h * 512:(h + 1) * 512],
                                 start=True, stop=True).then_inc(inp_ps, 1)
            transpose_qk(0, 0)
            transpose_qk(0, 1)
            scores(0, 0)
            pe.wait_ge(u_done, EB)
            pe.wait_ge(rope_mul, 8)
            pe.wait_ge(v_copied, 4)
            for h in range(2):
                for e in range(EB):
                    last = nc.tensor.matmul(ps_p[0:XR, h, :], xproj[:, e, :], u_s[:, e, h * 512:(h + 1) * 512],
                                            start=(e == 0), stop=(e == EB - 1))
                last.then_inc(xdbl_ps, 1)
            pe.wait_ge(xdbl_sb, 2)
            pe.wait_ge(qkt_copied, 4)
            for e in range(EB):
                for h in range(2):
                    if e == 1:
                        pe.wait_ge(dt_v, h + 1)
                    nc.tensor.matmul(ps_r[:, h, :], dtproj[:, e * P:(e + 1) * P], xdbl[0:DR, h * 512:(h + 1) * 512],
                                     start=True, stop=True).then_inc(dt_ps, 1)
            pe.wait_ge(dt_v, 2 * EB)
            project(0, 2)

            def batch(b, last):
                for g in range(KVH):
                    if not (last and g + 1 >= KVH):
                        scores(b, g + 1)
                    transpose_p(b, g, not (last and g + 1 >= KVH))
                    values(b, g)
                    if not (last and g + 2 >= KVH):
                        transpose_qk(b, g + 2)
                    if not (last and g + 3 >= KVH):
                        project(b, g + 3)
                out_project(b)

            with pe.Fori(0, LAST) as b:
                batch(b, False)
            batch(LAST, True)

            def transpose_gz(b):
                pe.wait_ge(gz_done, b + 1)
                if isinstance(b, int) and b == 0:
                    pe.wait_ge(pt_dve, 1 + UNITS)
                    pe.wait_ge(pt_act, 1 + 2 * UNITS)
                else:
                    pe.wait_ge(x2_done, b)
                for lt in range(TB):
                    for et in range(EB):
                        last = nc.tensor.transpose(ps_r[:, 0, lt * HID + et * P:lt * HID + (et + 1) * P],
                                                   gz[:, et, lt * P:(lt + 1) * P], ident[:])
                last.then_inc(gt_ps, 1)

            def transpose_x2(b):
                pe.wait_ge(xh2_done, b * TB + TB)
                if not (isinstance(b, int) and b == 0):
                    pe.wait_ge(x2t_sb, b)
                for k in range(KT):
                    for t in range(TB):
                        last = nc.tensor.transpose(ps_r[:, 1, k * S + t * P:k * S + (t + 1) * P],
                                                   xh2[:, t, k * P:(k + 1) * P], ident[:])
                last.then_inc(x2t_ps, 1)

            def gate_up(b):
                pe.wait_ge(x2t_sb, b + 1)
                for i in range(HT):
                    m = HP[i]
                    if not (isinstance(b, int) and b == 0 and i < 3):
                        pe.wait_ge(hid_done, b * HT + i - 2)
                    for w in range(2):
                        for k in range(KT):
                            last = nc.tensor.matmul(ps_s[0:m, i % 3, w * S:(w + 1) * S],
                                                    wgu[:, w, k, i * P:i * P + m], xh2_t[:, k, :],
                                                    start=(k == 0), stop=(k == KT - 1))
                    last.then_inc(gu_ps, 1)

            def down(b):
                pe.wait_ge(hid_done, b * HT + HT)
                if not (isinstance(b, int) and b == 0):
                    pe.wait_ge(res_done, b)
                for t in range(TB):
                    for i in range(HT):
                        m = HP[i]
                        last = nc.tensor.matmul(ps_p[:, t, 0:HID], hid_t[0:m, i, t * P:(t + 1) * P],
                                                wdn[0:m, i, :], start=(i == 0), stop=(i == HT - 1))
                    last.then_inc(dn_ps, 1)

            def ffn(b, last):
                if not last:
                    transpose_gz(b + 1)
                gate_up(b)
                down(b)
                if not last:
                    transpose_x2(b + 1)

            pe.wait_ge(wq_done, 1 + HT)
            transpose_gz(0)
            transpose_x2(0)
            ffn(0, False)
            with pe.Fori(1, LAST) as b:
                ffn(b, False)
            ffn(LAST, True)


def kernel(x, ctx_1024, L0_attn_Wq, L0_attn_Wk, L0_attn_Wv, L0_attn_Wo, L0_xattn_in_proj_w, L0_xattn_conv_w,
           L0_xattn_conv_b, L0_xattn_x_proj_w, L0_xattn_dt_proj_w, L0_xattn_dt_proj_b, L0_xattn_A_log,
           L0_xattn_D, L0_ffn_wq_gate, L0_ffn_s_gate, L0_ffn_wq_up, L0_ffn_s_up, L0_ffn_wq_down,
           L0_ffn_s_down):
    import concourse.bacc as bacc
    from concourse.bass_utils import run_bass_kernel_spmd

    inv = (1.0 / (10000.0 ** (np.arange(0, HD, 2, dtype=np.float32) / np.float32(HD)))).astype(np.float32)
    freq = np.arange(S, dtype=np.float32)[:, None] * inv[None, :]
    cos, sin = np.cos(freq), np.sin(freq)
    scale = np.repeat(np.array([HD ** -0.5] * GRP + [1.0], np.float32), HD)
    cos_t = (np.tile(cos, (1, 2 * (GRP + 1))) * scale).astype(np.float32)
    sin_t = (np.tile(np.concatenate([-sin, sin], 1), (1, GRP + 1)) * scale).astype(np.float32)

    rows = [np.asarray(w).reshape(KVH, -1, HID) for w in (L0_attn_Wq, L0_attn_Wk, L0_attn_Wv)]
    column = lambda v: np.asarray(v).reshape(DI, -1)
    arrays = {
        "x": np.asarray(x).reshape(L, HID),
        "ctx_t": np.asarray(ctx_1024).reshape(L, DM).T,
        "wqkv_t": np.concatenate(rows, 1).transpose(2, 0, 1),
        "wo_t": np.asarray(L0_attn_Wo).T,
        "cos_t": cos_t,
        "sin_t": sin_t,
        "inproj_t": np.asarray(L0_xattn_in_proj_w).T,
        "ssm_par": np.concatenate([column(v) for v in (L0_xattn_conv_w, L0_xattn_conv_b, L0_xattn_dt_proj_b,
                                                       L0_xattn_D, L0_xattn_A_log)], 1),
        "xproj_t": np.asarray(L0_xattn_x_proj_w).T,
        "dtproj_t": np.asarray(L0_xattn_dt_proj_w).T,
        "wgate_t": np.asarray(L0_ffn_wq_gate).T,
        "wup_t": np.asarray(L0_ffn_wq_up).T,
        "wdown_t": np.asarray(L0_ffn_wq_down).T,
        "s_gate": np.asarray(L0_ffn_s_gate),
        "s_up": np.asarray(L0_ffn_s_up),
        "s_down": np.asarray(L0_ffn_s_down),
    }
    arrays = {k: np.ascontiguousarray(v) for k, v in arrays.items()}
    nc = bacc.Bacc("TRN2", target_bir_lowering=False, num_devices=1)
    args = [nc.dram_tensor(k, v.shape, mybir.dt.from_np(v.dtype), kind="ExternalInput").ap()
            for k, v in arrays.items()]
    bc_scratch = nc.dram_tensor("bc_scratch", (2 * NS, L), F32, kind="Internal").ap()
    out = nc.dram_tensor("out", (B, S, HID), F32, kind="ExternalOutput").ap()
    decoder_layer(nc, *args, bc_scratch, out)
    r = run_bass_kernel_spmd(nc, [arrays], core_ids=[0])
    return r.results[0]["out"]
```

```python
from contextlib import ExitStack

import numpy as np

import concourse.bass as bass
from concourse import mybir

F32 = mybir.dt.float32
BF16 = mybir.dt.bfloat16
I32 = mybir.dt.int32
ALU = mybir.AluOpType
ACT = mybir.ActivationFunctionType
AX = mybir.AxisListType

P = 128
B, S, HID = 4, 256, 256
H, KVH, HD = 32, 8, 64
GRP = H // KVH
TB = S // P
KT = HID // P
UNITS = B * KVH
ROT = (GRP + 1) * HD
QKC = ROT + HD
GC = (GRP + 2) * HD
NS = 16
DM = 128
DI = 256
EB = DI // P
DC = 4
DR = 8
XR = DR + 2 * NS
L = B * S
HF = 704
HT = -(-HF // P)
HP = [min(P, HF - P * i) for i in range(HT)]
EPS = 1e-5
ZERO_POINT = 128.0
MASKED = -3.0e38
LAG = 4
LAST_SCANS = [1, 2, 2, 2, 2, 2, 1, 0]
NPAR = DC + 3 + NS


def decoder_layer(nc, x, ctx_t, wqkv_t, wo_t, cos_t, sin_t, inproj_t, ssm_par, xproj_t, dtproj_t,
                  wgate_t, wup_t, wdown_t, s_gate, s_up, s_down, bc_scratch, out):
    ctx = ExitStack()
    with ctx:
        def sb(name, shape, dt=F32):
            return ctx.enter_context(nc.sbuf_tensor(name, shape, dt))

        def sem(name):
            return ctx.enter_context(nc.semaphore(name))

        wqkv = sb("wqkv", [P, KT, KVH, GC])
        wo = sb("wo", [P, H // 2, HID])
        wgu_i = sb("wgu_i", [P, 2, KT, HF], I32)
        wgu = wgu_i[:].bitcast(F32)
        wdn_i = sb("wdn_i", [P, HT, HID], I32)
        wdn = wdn_i[:].bitcast(F32)
        sgu = sb("sgu", [P, 2, HT])
        sdn = sb("sdn", [P, HID])
        cos_s = sb("cos_s", [P, TB, ROT])
        sin_s = sb("sin_s", [P, TB, ROT])
        xs = sb("xs", [P, B * TB, HID])
        x1 = sb("x1", [P, B * TB, HID])
        xt_all = sb("xt_all", [P, KT, L])
        xt = sb("xt", [P, KT, S])
        stats = sb("stats", [P, B * TB, 6])
        mv = sb("mv", [P, B * TB, 2])
        rstd = sb("rstd", [P, B * TB])
        mv1 = sb("mv1", [P, B * TB, 2])
        rstd1 = sb("rstd1", [P, B * TB])
        nmr1 = sb("nmr1", [P, B * TB])
        mv2 = sb("mv2", [P, TB, 2])
        rstd2 = sb("rstd2", [P, TB])
        half = sb("half", [P, B * TB])
        eps = sb("eps", [P, TB])
        ident = sb("ident", [P, P])
        ident_b = sb("ident_b", [P, P], BF16)
        mask_diag = sb("mask_diag", [P, GRP * P], BF16)
        ropec = sb("ropec", [P, TB, ROT])
        ropes = sb("ropes", [P, TB, ROT])
        qkn = sb("qkn", [P, 2, TB, QKC])
        qkt = sb("qkt", [P, 2, 3, S])
        vv = sb("vv", [P, 4, TB, HD])
        nmax = sb("nmax", [P, 2, 2 * GRP])
        rsum = sb("rsum", [P, 2, 2 * GRP])
        rinv = sb("rinv", [P, 2, 2 * GRP])
        prob0 = sb("prob0", [P, 2, GRP, P])
        prob1 = sb("prob1", [P, 2, GRP, S])
        pt = sb("pt", [P, 3, 4 * P])
        attn_t = sb("attn_t", [P, H // 2, S])
        par = sb("par", [P, EB, NPAR])
        a_neg = sb("a_neg", [P, EB, NS])
        a_exp = sb("a_exp", [P, EB, NS])
        inproj = sb("inproj", [P, DI])
        xproj = sb("xproj", [P, EB, XR])
        dtproj = sb("dtproj", [DR, DI])
        delta = sb("delta", [P, EB, L])
        du = sb("du", [P, EB, L])
        y = sb("y", [P, EB, L])
        decay = sb("decay", [P, 2, L])
        state = sb("state", [P, 2, L])
        bc = sb("bc", [P, 2, 2, L])
        ctxs = bc[:, 0, 0, :]
        u_s = bc[:, 1, :, :]
        conv_in = attn_t[:].rearrange("p a s -> p (a s)")[:, 0:EB * B * (S + DC - 1)].rearrange(
            "p (e b s) -> p e b s", e=EB, b=B)
        xdbl = attn_t[:].rearrange("p a s -> p (a s)")[0:XR, 3 * L:4 * L]
        flat_n = qkn[:].rearrange("p r t n -> p (r t n)")
        flat_t = qkt[:].rearrange("p r k s -> p (r k s)")
        sz = flat_n[:, 0:TB * HID].rearrange("p (t n) -> p t n", t=TB)
        gz = flat_n[:, TB * HID:2 * TB * HID].rearrange("p (t n) -> p t n", t=TB)
        xh2 = flat_t[:, 0:TB * HID].rearrange("p (t n) -> p t n", t=TB)
        xh2_t = flat_t[:, TB * HID:2 * TB * HID].rearrange("p (k n) -> p k n", k=KT)
        gate = ropec[:].rearrange("p t n -> p (t n)")[:, 0:2 * S].rearrange("p (r s) -> p r s", r=2)
        hid_t = prob1[:].rearrange("p a b s -> p (a b s)")[:, 0:HT * S].rearrange(
            "p (h s) -> p h s", h=HT)

        ps_s = ctx.enter_context(nc.psum_tensor("ps_s", [P, 3, 512], F32))
        ps_r = ctx.enter_context(nc.psum_tensor("ps_r", [P, 2, 512], F32))
        ps_p = ctx.enter_context(nc.psum_tensor("ps_p", [P, 2, 512], F32))
        ps_o = ctx.enter_context(nc.psum_tensor("ps_o", [P, 512], F32))

        x_in, ssm_in, wqkv_in, tab_in, wo_in, ffn_in = (
            sem(n) for n in ("x_in", "ssm_in", "wqkv_in", "tab_in", "wo_in", "ffn_in"))
        wqkv_in2, ctx_in, par_in = sem("wqkv_in2"), sem("ctx_in"), sem("par_in")
        bc_out, bc_in0, bc_in1, out_done = (sem(n) for n in ("bc_out", "bc_in0", "bc_in1", "out_done"))
        bc_in = [bc_in0, bc_in1]
        consts = sem("consts")
        ln_stat, ln_rstd, ln_x = sem("ln_stat"), sem("ln_rstd"), sem("ln_x")
        xt_ps, xt_sb, xt_ready = sem("xt_ps"), sem("xt_sb"), sem("xt_ready")
        v_chain, p_chain = sem("v_chain"), sem("p_chain")
        inp_ps, inp_sb, u_done = sem("inp_ps"), sem("inp_sb"), sem("u_done")
        conv_done0, conv_done1 = sem("conv_done0"), sem("conv_done1")
        xdbl_ps, xdbl_sb, dt_ps, dt_v = sem("xdbl_ps"), sem("xdbl_sb"), sem("dt_ps"), sem("dt_v")
        sp_e, sp_w, sp_l, a_done = sem("sp_e"), sem("sp_w"), sem("sp_l"), sem("a_done")
        sp_c = sem("sp_c")
        ssm_ready = sem("ssm_ready")
        proj_done = sem("proj_done")
        qkt_done = sem("qkt_done")
        score_done = sem("score_done")
        even_done = sem("even_done")
        pt_done = sem("pt_done")
        pv_done = sem("pv_done")
        wo_done = sem("wo_done")
        rope_mul = sem("rope_mul")
        v_copied = sem("v_copied")
        nmax_done = sem("nmax_done")
        rinv_done = sem("rinv_done")
        pt_dve = sem("pt_dve")
        pt_act = sem("pt_act")
        qkt_copied = sem("qkt_copied")
        exp_done = sem("exp_done")
        attn_copied = sem("attn_copied")
        rope_add = sem("rope_add")
        norm_done = sem("norm_done")
        decay_done = sem("decay_done")
        decay_free = sem("decay_free")
        drive_done = sem("drive_done")
        hc_done = sem("hc_done")
        state_free = sem("state_free")
        x1_done = sem("x1_done")
        st1_done = sem("st1_done")
        r1_done = sem("r1_done")
        sz_done, gz_done = sem("sz_done"), sem("gz_done")
        gt_ps, x2_done, st2_done, r2_done = sem("gt_ps"), sem("x2_done"), sem("st2_done"), sem("r2_done")
        xh2_done, x2t_ps, x2t_sb = sem("xh2_done"), sem("x2t_ps"), sem("x2t_sb")
        bn2_done = sem("bn2_done")
        gu_ps, gate_done, hid_done = sem("gu_ps"), sem("gate_done"), sem("hid_done")
        dn_ps, res_done = sem("dn_ps"), sem("res_done")
        wq_done = sem("wq_done")

        LAST = B - 1

        def scans(b, g):
            if g < 0:
                return [(b, g - LAG)]
            if isinstance(b, int) and b == LAST:
                at = sum(LAST_SCANS[:g]) - LAG
                return [(b, at + i) for i in range(LAST_SCANS[g])]
            return [(b, g - LAG)] if not isinstance(b, int) or b * KVH + g >= LAG else []

        mulof = lambda v, k: k * v

        block = ctx.enter_context(nc.Block())

        @block.sync
        def _(sp):
            sp.dma_start(xs[:], x.rearrange("(t p) n -> p t n", p=P)).then_inc(x_in, 16)
            sp.dma_start(xproj[:], xproj_t.rearrange("(e p) n -> p e n", p=P)).then_inc(ssm_in, 16)
            sp.dma_start(dtproj[:], dtproj_t).then_inc(ssm_in, 16)
            w = wqkv_t.rearrange("(k p) g n -> p k g n", p=P)
            sp.dma_start(wqkv[:, :, 0:2, :], w[:, :, 0:2, :]).then_inc(wqkv_in, 16)
            sp.dma_start(cos_s[:], cos_t.rearrange("(t p) n -> p t n", p=P)).then_inc(tab_in, 16)
            sp.dma_start(sin_s[:], sin_t.rearrange("(t p) n -> p t n", p=P)).then_inc(tab_in, 16)
            sp.dma_start(wqkv[:, :, 2:KVH, :], w[:, :, 2:KVH, :]).then_inc(wqkv_in2, 16)
            sp.wait_ge(xdbl_sb, 2)
            sp.dma_start(bc_scratch, xdbl[DR:XR, :]).then_inc(bc_out, 16)
            sp.wait_ge(bc_out, 16)

            def load_bc(n):
                for c in range(2):
                    sp.dma_start(bc[:, n, c, :], bc_scratch[c * NS + n:c * NS + n + 1, :].to_broadcast([P, L])
                                 ).then_inc(bc_in[n], 16)

            load_bc(0)
            sp.dma_start(wo[:], wo_t.rearrange("(k p) n -> p k n", p=P)).then_inc(wo_in, 16)
            for i, w in enumerate((wgate_t, wup_t)):
                sp.dma_start(wgu_i[:, i, :, :], w.rearrange("(k p) n -> p k n", p=P)).then_inc(ffn_in, 16)
            full = P * (HT - 1)
            sp.dma_start(wdn_i[:, 0:HT - 1, :], wdown_t[0:full, :].rearrange("(k p) n -> p k n", p=P)
                         ).then_inc(ffn_in, 16)
            sp.dma_start(wdn_i[0:HP[-1], HT - 1, :], wdown_t[full:HF, :]).then_inc(ffn_in, 16)
            for i, s in enumerate((s_gate, s_up)):
                with nc.allow_non_contiguous_dma(reason="704 scales, once"):
                    sp.dma_start(sgu[:, i, 0:HT - 1], s[0:full].rearrange("(k p) -> p k", p=P)
                                 ).then_inc(ffn_in, 16)
                    sp.dma_start(sgu[0:HP[-1], i, HT - 1:HT], s[full:HF].rearrange("(p k) -> p k", k=1)
                                 ).then_inc(ffn_in, 16)
            sp.dma_start(sdn[:], s_down.rearrange("(a n) -> a n", a=1).to_broadcast([P, HID])
                         ).then_inc(ffn_in, 16)
            sp.wait_ge(ssm_ready, 5)
            load_bc(1)
            with sp.Fori(0, NS // 2 - 1) as j:
                for k in range(2):
                    sp.wait_ge(hc_done, j * 4 + 2 * k + 2)
                    for c in range(2):
                        sp.dma_start(bc[:, k, c, :],
                                     bc_scratch[bass.ds(j * 2 + (c * NS + k + 2), 1), :].to_broadcast([P, L])
                                     ).then_inc(bc_in[k], 16)
            with sp.Fori(0, B) as b:
                sp.wait_ge(res_done, b + 1)
                sp.dma_start(out[bass.ds(b, 1), :, :].rearrange("b (t p) n -> p (b t) n", p=P),
                             x1[:, bass.ds(b * TB, TB), :]).then_inc(out_done, 16)
            sp.wait_ge(out_done, 16 * B)

        @block.gpsimd
        def _(pool):
            pool.sem_inc(norm_done, 1)
            nc.gpsimd.memset(half[:], -0.5).then_inc(consts, 1)
            nc.gpsimd.memset(eps[:], EPS).then_inc(consts, 1)
            nc.gpsimd.memset(ident[:], 0.0).then_inc(consts, 1)
            nc.gpsimd.memset(ident_b[:], 0.0).then_inc(consts, 1)
            nc.gpsimd.memset(mask_diag[:], 0.0).then_inc(consts, 1)
            nc.gpsimd.memset(conv_in[:, :, :, 0:DC - 1], 0.0).then_inc(consts, 1)
            pool.wait_ge(consts, 6)
            for m in (ident, ident_b):
                nc.gpsimd.affine_select(out=m[:], in_=m[:], compare_op=ALU.not_equal, fill=1.0, base=0,
                                        pattern=[[-1, P]], channel_multiplier=1).then_inc(consts, 1)
            m0 = mask_diag[:].rearrange("p (h k) -> p h k", h=GRP)
            nc.gpsimd.affine_select(out=m0, in_=m0, compare_op=ALU.is_ge, fill=MASKED, base=0,
                                    pattern=[[0, GRP], [-1, P]], channel_multiplier=1).then_inc(consts, 1)
            pool.wait_ge(ln_stat, B * TB)
            nc.gpsimd.tensor_scalar(rstd[:], mv[:, :, 1], EPS, 1.0, ALU.add, ALU.mult).then_inc(p_chain, 1)
            pool.wait_ge(p_chain, 1)
            nc.gpsimd.tensor_tensor(rstd[:], rstd[:], half[:], ALU.pow).then_inc(ln_rstd, 1)
            by_batch = lambda v: v.rearrange("p (b s) -> p b s", b=B)
            acc, tap = by_batch(du[:, 1, :]), by_batch(y[:, 1, :])
            pool.wait_ge(par_in, 16)
            pool.wait_ge(inp_sb, 2 * EB)
            nc.gpsimd.tensor_scalar(acc, conv_in[:, 1, :, 0:S], par[:, 1, 0:1], par[:, 1, DC:DC + 1],
                                    ALU.mult, ALU.add).then_inc(conv_done1, 1)
            for j in range(1, DC):
                if j > 1:
                    pool.wait_ge(conv_done1, 2 * j - 1)
                nc.gpsimd.tensor_scalar(tap, conv_in[:, 1, :, j:j + S], par[:, 1, j:j + 1], 1.0,
                                        ALU.mult, ALU.mult).then_inc(conv_done1, 1)
                pool.wait_ge(conv_done1, 2 * j)
                nc.gpsimd.tensor_tensor(acc, acc, tap, ALU.add).then_inc(conv_done1, 1)
            nc.gpsimd.memset(rsum[:], 0.0).then_inc(state_free, 1)
            nc.gpsimd.memset(rinv[:], 0.0).then_inc(state_free, 1)

            def add_rope(b, g):
                u = mulof(b, KVH) + g
                for t in range(TB):
                    pool.wait_ge(rope_mul, u * 4 + 2 * (t + 1))
                    if t == 0 and not (isinstance(b, int) and 8 * b + g < 2):
                        pool.wait_ge(qkt_done, u * 2 - 2)
                    o = qkn[:, g % 2, t, :]
                    nc.gpsimd.tensor_tensor(o[:, 0:ROT], ropec[:, t, :], ropes[:, t, :], ALU.add
                                            ).then_inc(rope_add, 1)
                    nc.gpsimd.tensor_tensor(o[:, ROT:QKC], ropec[:, t, ROT - HD:], ropes[:, t, ROT - HD:],
                                            ALU.add).then_inc(rope_add, 1)

            def normalise(b, g):
                u = mulof(b, KVH) + g
                pool.wait_ge(consts, 9)
                pool.wait_ge(rinv_done, u + 1)
                for h in range(GRP):
                    nc.gpsimd.tensor_scalar(prob0[:, g % 2, h, :], prob0[:, g % 2, h, :],
                                            rinv[:, g % 2, h:h + 1], 1.0, ALU.mult, ALU.mult
                                            ).then_inc(norm_done, 1)
                for h in range(GRP):
                    nc.gpsimd.tensor_scalar(prob1[:, g % 2, h, :], prob1[:, g % 2, h, :],
                                            rinv[:, g % 2, GRP + h:GRP + h + 1], 1.0, ALU.mult, ALU.mult
                                            ).then_inc(norm_done, 1)

            def add_y(b, g):
                u = mulof(b, KVH) + g
                pool.wait_ge(hc_done, u + 1)
                pool.wait_ge(state_free, u + 1)
                nc.gpsimd.tensor_tensor(y[:, g % 2, :], y[:, g % 2, :], state[:, g % 2, :], ALU.add
                                        ).then_inc(state_free, 1)

            add_rope(0, 0)
            add_rope(0, 1)
            normalise(0, 0)

            def x1_rstd(lo, hi, step):
                r = rstd1[:, lo * TB:hi * TB]
                pool.wait_ge(st1_done, hi * TB)
                nc.gpsimd.tensor_scalar(r, mv1[:, lo * TB:hi * TB, 1], EPS, 1.0, ALU.add, ALU.mult
                                        ).then_inc(p_chain, 1)
                pool.wait_ge(p_chain, step)
                nc.gpsimd.tensor_tensor(r, r, half[:, lo * TB:hi * TB], ALU.pow).then_inc(r1_done, 1)

            def batch(b, first, last):
                for g in range(KVH):
                    if not (last and g + 2 >= KVH):
                        add_rope(b, g + 2)
                    if not (first and g == 0):
                        for v in scans(b, g - 1):
                            add_y(*v)
                    if not (last and g + 1 >= KVH):
                        normalise(b, g + 1)
                    if last and g == 2:
                        x1_rstd(0, LAST, 2)

            batch(0, True, False)
            with pool.Fori(1, LAST) as b:
                batch(b, False, False)
            batch(LAST, False, True)

            def ffn_rstd(b):
                pool.wait_ge(st2_done, mulof(b, TB) + TB)
                nc.gpsimd.tensor_tensor(rstd2[:], mv2[:, :, 1], eps[:], ALU.add).then_inc(p_chain, 1)
                pool.wait_ge(p_chain, b + (4 if not isinstance(b, int) else 3))
                nc.gpsimd.tensor_tensor(rstd2[:], rstd2[:], half[:, 0:TB], ALU.pow).then_inc(r2_done, 1)

            ffn_rstd(0)
            x1_rstd(LAST, B, 4)
            with pool.Fori(1, B) as b:
                ffn_rstd(b)

        @block.scalar
        def _(act):
            def copy_qkt(b, g):
                u = mulof(b, KVH) + g
                slot = g - 2
                for t in range(TB):
                    act.wait_ge(qkt_done, u * 2 + t + 1)
                    bank = (5 * slot + 3 + t) % 2
                    nc.scalar.activation(qkt[:, g % 2, :, t * P:(t + 1) * P],
                                         ps_r[:, bank, 0:3 * P].rearrange("p (k s) -> p k s", k=3), ACT.Copy
                                         ).then_inc(qkt_copied, 1)

            def exps(b, g, part):
                u = mulof(b, KVH) + g
                act.wait_ge(nmax_done, u * 3 + 3 - part)
                r = g % 2
                for k in range(GRP if part == 0 else 2):
                    if part == 0:
                        o, i, c = prob0[:, r, k, :], ps_s[:, 0, k * P:(k + 1) * P], k
                    else:
                        c = GRP + 2 * (part - 1) + k
                        o, i = prob1[:, r, c - GRP, :], ps_s[:, part, k * S:(k + 1) * S]
                    nc.scalar.activation(o, i, ACT.Exp, bias=nmax[:, r, c:c + 1],
                                         accum_out=rsum[:, r, c:c + 1]).then_inc(exp_done, 1)

            def copy_pt(b, g, fill):
                u = mulof(b, KVH) + g
                act.wait_ge(pt_done, u * 3 + fill + 1)
                nc.scalar.activation(pt[:, fill, :], ps_r[:, (5 * g + fill) % 2, :], ACT.Copy
                                     ).then_inc(pt_act, 1)

            def copy_attn(b, g):
                u = mulof(b, KVH) + g
                act.wait_ge(pv_done, u + 1)
                if g == 0 and not (isinstance(b, int) and b == 0):
                    act.wait_ge(wo_done, b + 1)
                nc.scalar.activation(attn_t[:, 2 * g:2 * g + 2, :],
                                     ps_o[:].rearrange("p (k s) -> p k s", k=2), ACT.Copy
                                     ).then_inc(attn_copied, 1)

            def decays(b, g):
                u = mulof(b, KVH) + g
                n = b * (KVH // 2) + g // 2
                act.wait_ge(decay_free, u + 1)
                nc.scalar.activation(
                    decay[:, g % 2, :].rearrange("p (b s) -> p b s", b=B)[:, :, 1:],
                    delta[:, g % 2, :].rearrange("p (b s) -> p b s", b=B)[:, :, 1:],
                    ACT.Exp, scale=a_neg[:, g % 2, bass.ds(n, 1)]).then_inc(decay_done, 1)

            nc.scalar.dma_start(inproj[:], inproj_t).then_inc(ctx_in, 16)
            nc.scalar.dma_start(ctxs, ctx_t).then_inc(ctx_in, 16)
            nc.scalar.dma_start(par[:], ssm_par.rearrange("(e p) n -> p e n", p=P)).then_inc(par_in, 16)
            act.sem_inc(pt_act, 1)
            act.sem_inc(attn_copied, 1)
            act.wait_ge(consts, 6)
            for i in range(2 * EB):
                e, h = divmod(i, 2)
                act.wait_ge(inp_ps, i + 1)
                src = ps_s[:, i, :] if i < 3 else ps_o[:]
                nc.scalar.activation(conv_in[:, e, 2 * h:2 * h + 2, DC - 1:],
                                     src.rearrange("p (b s) -> p b s", b=2), ACT.Copy).then_inc(inp_sb, 1)
            for i in range(B):
                act.wait_ge(xt_ps, i + 1)
                nc.scalar.activation(xt_all[:, :, i * S:(i + 1) * S],
                                     (ps_r[:, i % 2, :]).rearrange("p (k s) -> p k s", k=KT), ACT.Copy
                                     ).then_inc(xt_sb, 1)
            for e, (done, n) in enumerate(((conv_done0, DC), (conv_done1, 2 * DC - 1))):
                act.wait_ge(done, n)
                nc.scalar.activation(u_s[:, e, :], du[:, e, :], ACT.Silu).then_inc(u_done, 1)
            copy_qkt(0, 0)
            copy_qkt(0, 1)
            for i in range(2):
                act.wait_ge(xdbl_ps, i + 1)
                nc.scalar.activation(xdbl[:, i * 512:(i + 1) * 512], ps_p[0:XR, i, :], ACT.Copy
                                     ).then_inc(xdbl_sb, 1)
            for part in (2, 1, 0):
                exps(0, 0, part)
            nc.scalar.activation(a_exp[:], par[:, :, DC + 3:], ACT.Exp).then_inc(a_done, 1)

            def prepare_scan(g):
                for e in range(EB):
                    if g == 0:
                        act.wait_ge(dt_v, 2 * (e + 1))
                        nc.scalar.activation(decay[:, e, :], delta[:, e, :], ACT.Abs).then_inc(sp_e, 1)
                        act.wait_ge(sp_e, 2 * e + 1)
                        nc.scalar.activation(decay[:, e, :], decay[:, e, :], ACT.Exp, scale=-1.0
                                             ).then_inc(sp_e, 1)
                    elif g == 1:
                        act.wait_ge(sp_w, e + 1)
                        nc.scalar.activation(y[:, e, :], state[:, e, :], ACT.Ln).then_inc(sp_l, 1)
                if g == LAG - 1:
                    act.wait_ge(ssm_ready, 5)

            act.wait_ge(bc_out, 16)

            def batch(b, first, last):
                for g in range(KVH):
                    copy_pt(b, g, 0)
                    nxt = not (last and g + 1 >= KVH)
                    if nxt:
                        exps(b, g + 1, 2)
                    copy_pt(b, g, 2)
                    if nxt:
                        exps(b, g + 1, 1)
                        exps(b, g + 1, 0)
                    if not (last and g + 2 >= KVH):
                        copy_qkt(b, g + 2)
                    copy_attn(b, g)
                    if first and g < LAG:
                        prepare_scan(g)
                    if last:
                        for v in scans(b, g + 1) if g + 1 < KVH else []:
                            decays(*v)
                        if g == KVH - 2:
                            act.wait_ge(r1_done, 2)
                            silu_z(0)
                    elif not first or g + 1 >= LAG:
                        decays(b, g + 1 - LAG)

            def silu_z(b):
                if not (isinstance(b, int) and b == 0):
                    act.wait_ge(gz_done, b)
                for t in range(TB):
                    nc.scalar.activation(sz[:, t, :], x1[:, bass.ds(b * TB + t, 1), :], ACT.Silu,
                                         bias=nmr1[:, bass.ds(b * TB + t, 1)],
                                         scale=rstd1[:, bass.ds(b * TB + t, 1)]).then_inc(sz_done, 1)

            def copy_x2t(b):
                act.wait_ge(x2t_ps, b + 1)
                nc.scalar.activation(xh2_t, ps_r[:, 1, :].rearrange("p (k s) -> p k s", k=KT),
                                     ACT.Copy).then_inc(x2t_sb, 1)

            def gates(b):
                for i in range(HT):
                    act.wait_ge(gu_ps, b * HT + i + 1)
                    if not (isinstance(b, int) and b == 0 and i < 2):
                        act.wait_ge(hid_done, b * HT + i - 1)
                    m = HP[i]
                    nc.scalar.activation(gate[0:m, i % 2, :], ps_s[0:m, i % 3, 0:S], ACT.Silu,
                                         scale=sgu[0:m, 0, i:i + 1]).then_inc(gate_done, 1)

            def ffn(b, last):
                if not last:
                    silu_z(b + 1)
                gates(b)
                if not last:
                    copy_x2t(b + 1)

            batch(0, True, False)
            with act.Fori(1, LAST) as b:
                batch(b, False, False)
            batch(LAST, False, True)

            copy_x2t(0)
            act.wait_ge(ffn_in, 16 * 9)
            ffn(0, False)
            act.wait_ge(r1_done, 4)
            with act.Fori(1, LAST) as b:
                ffn(b, False)
            ffn(LAST, True)

        @block.vector
        def _(dve):
            chain = [0]

            def then(ins):
                chain[0] += 1
                ins.then_inc(v_chain, 1)
                dve.wait_ge(v_chain, chain[0])

            dve.sem_inc(pt_dve, 1)
            dve.sem_inc(x1_done, 1)
            dve.wait_ge(x_in, 16)
            for i in range(B * TB):
                nc.vector.bn_stats(stats[:, i, :], xs[:, i, :]).then_inc(v_chain, 1)
            chain[0] += B * TB
            dve.wait_ge(v_chain, chain[0])
            for i in range(B * TB):
                nc.vector.bn_aggr(mv[:, i, :], stats[:, i, :]).then_inc(ln_stat, 1)
            dve.wait_ge(ln_rstd, 1)
            dve.wait_ge(ln_stat, B * TB)
            for i in range(B * TB):
                nc.vector.tensor_scalar(x1[:, i, :], xs[:, i, :], mv[:, i, 0:1], rstd[:, i:i + 1],
                                        ALU.subtract, ALU.mult).then_inc(ln_x, 1)
            dve.wait_ge(xt_sb, 1)
            nc.vector.tensor_copy(xt[:], xt_all[:, :, 0:S]).then_inc(xt_ready, 1)

            def rope(b, g):
                u = mulof(b, KVH) + g
                for t in range(TB):
                    dve.wait_ge(proj_done, u * 2 + t + 1)
                    if not (isinstance(b, int) and 8 * b + g < 1):
                        dve.wait_ge(rope_add, u * 4 - 2 * (TB - 1 - t))
                    q = ps_p[:, t, 0:ROT]
                    nc.vector.tensor_tensor(ropec[:, t, :], q, cos_s[:, t, :], ALU.mult).then_inc(rope_mul, 1)
                    swapped = q.rearrange("p (h two d) -> p h two d", two=2, d=HD // 2)[:, :, ::-1, :]
                    nc.vector.tensor_tensor(
                        ropes[:, t, :].rearrange("p (h two d) -> p h two d", two=2, d=HD // 2), swapped,
                        sin_s[:, t, :].rearrange("p (h two d) -> p h two d", two=2, d=HD // 2),
                        ALU.mult).then_inc(rope_mul, 1)
                    nc.vector.tensor_copy(vv[:, g % 4, t, :], ps_p[:, t, ROT:GC]).then_inc(v_copied, 1)

            def negmax(b, g):
                u = mulof(b, KVH) + g
                for part in (2, 1, 0):
                    dve.wait_ge(score_done, u * 3 + 3 - part)
                    k, c = (GRP, 0) if part == 0 else (2, GRP + 2 * (part - 1))
                    nc.vector.tensor_reduce(nmax[:, g % 2, c:c + k],
                                            ps_s[:, part, :].rearrange("p (k s) -> p k s", k=k),
                                            AX.X, ALU.max, negate=True).then_inc(nmax_done, 1)

            def reciprocals(b, g):
                u = mulof(b, KVH) + g
                dve.wait_ge(exp_done, u * 8 + 8)
                if not (isinstance(b, int) and 8 * b + g < 2):
                    dve.wait_ge(norm_done, u * 8 - 7)
                nc.vector.reciprocal(rinv[:, g % 2, :], rsum[:, g % 2, :]).then_inc(rinv_done, 1)

            dve.wait_ge(par_in, 16)
            dve.wait_ge(inp_sb, 2)
            acc = du[:, 0, :].rearrange("p (b s) -> p b s", b=B)
            nc.vector.tensor_scalar(acc, conv_in[:, 0, :, 0:S], par[:, 0, 0:1], par[:, 0, DC:DC + 1],
                                    ALU.mult, ALU.add).then_inc(conv_done0, 1)
            for j in range(1, DC):
                dve.wait_ge(conv_done0, j)
                nc.vector.scalar_tensor_tensor(acc, conv_in[:, 0, :, j:j + S], par[:, 0, j:j + 1], acc,
                                               ALU.mult, ALU.add).then_inc(conv_done0, 1)
            dve.wait_ge(tab_in, 32)
            rope(0, 0)
            rope(0, 1)
            negmax(0, 0)
            for e in range(EB):
                for h in range(2):
                    dve.wait_ge(dt_ps, 2 * e + h + 1)
                    nc.vector.tensor_scalar(delta[:, e, h * 512:(h + 1) * 512], ps_r[:, h, :],
                                            par[:, e, DC + 1:DC + 2], None, ALU.add).then_inc(dt_v, 1)
            reciprocals(0, 0)

            def prepare_scan(g):
                if g == 1:
                    dve.wait_ge(a_done, 1)
                    nc.vector.tensor_scalar(a_neg[:], a_exp[:], -1.0, None, ALU.mult).then_inc(ssm_ready, 1)
                    for e in range(EB):
                        dve.wait_ge(sp_e, 2 * (e + 1))
                        nc.vector.tensor_scalar(state[:, e, :], decay[:, e, :], 1.0, None, ALU.add
                                                ).then_inc(sp_w, 1)
                    for e in range(EB):
                        dve.wait_ge(sp_w, e + 1)
                        nc.vector.scalar_tensor_tensor(decay[:, e, :], state[:, e, :], 1.0, decay[:, e, :],
                                                       ALU.subtract, ALU.subtract).then_inc(sp_c, 1)
                if g >= 2:
                    e = g - 2
                    dve.wait_ge(sp_c, e + 1)
                    dve.wait_ge(sp_l, e + 1)
                    then(nc.vector.tensor_tensor(y[:, e, :], y[:, e, :], decay[:, e, :], ALU.subtract))
                    then(nc.vector.scalar_tensor_tensor(delta[:, e, :], delta[:, e, :], 0.0, y[:, e, :],
                                                        ALU.max, ALU.add))
                    dve.wait_ge(u_done, e + 1)
                    nc.vector.tensor_tensor(du[:, e, :], delta[:, e, :], u_s[:, e, :], ALU.mult
                                            ).then_inc(ssm_ready, 1)
                    nc.vector.tensor_scalar(y[:, e, :], u_s[:, e, :], par[:, e, DC + 2:DC + 3], None, ALU.mult
                                            ).then_inc(ssm_ready, 1)
                    nc.vector.memset(decay[:, e, :].rearrange("p (b s) -> p b s", b=B)[:, :, 0:1], 0.0
                                     ).then_inc(decay_free, 1)

            def drive(b, g):
                u = mulof(b, KVH) + g
                n = b * (KVH // 2) + g // 2
                r = (g // 2) % 2
                dve.wait_ge(bc_in[r], (b * 2 + g // 4 + 1) * 32)
                dve.wait_ge(state_free, u + 1)
                nc.vector.tensor_tensor(state[:, g % 2, :], du[:, g % 2, :], bc[:, r, 0, :], ALU.mult
                                        ).then_inc(drive_done, 1)

            def scan(b, g):
                u = mulof(b, KVH) + g
                dve.wait_ge(drive_done, u + 1)
                dve.wait_ge(decay_done, u + 1)
                nc.vector.tensor_tensor_scan(state[:, g % 2, :], decay[:, g % 2, :], state[:, g % 2, :], 0.0,
                                             ALU.mult, ALU.add).then_inc(decay_free, 1)

            def times_c(b, g):
                u = mulof(b, KVH) + g
                dve.wait_ge(decay_free, u + 3)
                nc.vector.tensor_tensor(state[:, g % 2, :], state[:, g % 2, :],
                                        bc[:, (g // 2) % 2, 1, :], ALU.mult).then_inc(hc_done, 1)

            def copy_pt(b, g):
                u = mulof(b, KVH) + g
                dve.wait_ge(pt_done, u * 3 + 2)
                nc.vector.tensor_copy(pt[:, 1, :], ps_r[:, (5 * g + 1) % 2, :]).then_inc(pt_dve, 1)

            def next_x(b):
                dve.wait_ge(proj_done, b * 16 + 16)
                nc.vector.tensor_copy(xt[:], xt_all[:, :, bass.ds((b + 1) * S, S)]).then_inc(xt_ready, 1)

            def add_attention(b):
                dve.wait_ge(wo_done, b + 2)
                nc.vector.tensor_tensor(x1[:, bass.ds(b * TB, TB), :],
                                        ps_o[:].rearrange("p (t n) -> p t n", t=TB),
                                        xs[:, bass.ds(b * TB, TB), :], ALU.add).then_inc(x1_done, 1)

            def dequantise():
                dve.wait_ge(ffn_in, 16 * 9)
                nc.vector.tensor_scalar(wgu, wgu_i[:], ZERO_POINT, None, ALU.subtract).then_inc(wq_done, 1)
                for i in range(HT):
                    m = HP[i]
                    nc.vector.scalar_tensor_tensor(wdn[0:m, i, :], wdn_i[0:m, i, :], ZERO_POINT,
                                                   sdn[0:m, :], ALU.subtract, ALU.mult).then_inc(wq_done, 1)

            def x1_stats(lo, hi):
                dve.wait_ge(x1_done, 1 + hi)
                for i in range(lo * TB, hi * TB):
                    nc.vector.bn_stats(stats[:, i, :], x1[:, i, :]).then_inc(v_chain, 1)
                chain[0] += (hi - lo) * TB
                dve.wait_ge(v_chain, chain[0])
                for i in range(lo * TB, hi * TB):
                    nc.vector.bn_aggr(mv1[:, i, :], stats[:, i, :]).then_inc(st1_done, 1)

            def x1_nmr(lo, hi, step):
                dve.wait_ge(r1_done, step)
                nc.vector.scalar_tensor_tensor(nmr1[:, lo * TB:hi * TB], mv1[:, lo * TB:hi * TB, 0], -1.0,
                                               rstd1[:, lo * TB:hi * TB], ALU.mult, ALU.mult
                                               ).then_inc(r1_done, 1)

            def batch(b, first, last):
                for g in range(KVH):
                    if not (last and g + 2 >= KVH):
                        rope(b, g + 2)
                    if not (last and g + 1 >= KVH):
                        negmax(b, g + 1)
                    if g == 0 and not first:
                        add_attention(b - 1)
                    copy_pt(b, g)
                    units = scans(b, g)
                    if units:
                        drive(*units[0])
                        scan(*units[0])
                    if not (last and g + 1 >= KVH):
                        reciprocals(b, g + 1)
                    if units:
                        times_c(*units[0])
                    for v in units[1:]:
                        drive(*v)
                        scan(*v)
                        times_c(*v)
                    if first and g < LAG:
                        prepare_scan(g)
                    if g == 4 and not last:
                        next_x(b)
                    if last and g == 1:
                        x1_stats(0, LAST)
                    if last and g == 3:
                        x1_nmr(0, LAST, 1)
                    if last and g == KVH - 2:
                        dequantise()

            dve.wait_ge(xt_sb, B)
            batch(0, True, False)
            with dve.Fori(1, LAST) as b:
                batch(b, False, False)
            batch(LAST, False, True)

            dve.wait_ge(state_free, UNITS + 2)

            def gate_z(b):
                dve.wait_ge(sz_done, b * TB + TB)
                if not (isinstance(b, int) and b == 0):
                    dve.wait_ge(gt_ps, b)
                nc.vector.tensor_tensor(gz, y[:, :, bass.ds(b * S, S)], sz, ALU.mult).then_inc(gz_done, 1)

            def norm_x2(b):
                dve.wait_ge(gt_ps, b + 1)
                nc.vector.tensor_tensor(xs[:, bass.ds(b * TB, TB), :],
                                        ps_r[:, 0, :].rearrange("p (t n) -> p t n", t=TB),
                                        x1[:, bass.ds(b * TB, TB), :], ALU.add).then_inc(x2_done, 1)
                dve.wait_ge(x1_done, 2)
                dve.wait_ge(x2_done, b + 1)
                for t in range(TB):
                    nc.vector.bn_stats(stats[:, t, :], xs[:, bass.ds(b * TB + t, 1), :].rearrange(
                        "p a n -> p (a n)")).then_inc(bn2_done, 1)
                dve.wait_ge(x1_done, 2)
                dve.wait_ge(bn2_done, b * TB + TB)
                for t in range(TB):
                    nc.vector.bn_aggr(mv2[:, t, :], stats[:, t, :]).then_inc(st2_done, 1)
                dve.wait_ge(r2_done, b + 1)
                dve.wait_ge(st2_done, b * TB + TB)
                for t in range(TB):
                    nc.vector.tensor_scalar(xh2[:, t, :], xs[:, bass.ds(b * TB + t, 1), :], mv2[:, t, 0:1],
                                            rstd2[:, t:t + 1], ALU.subtract, ALU.mult).then_inc(xh2_done, 1)

            def hidden(b):
                for i in range(HT):
                    m = HP[i]
                    dve.wait_ge(gate_done, b * HT + i + 1)
                    if i == 0 and not (isinstance(b, int) and b == 0):
                        dve.wait_ge(dn_ps, b * TB)
                    nc.vector.scalar_tensor_tensor(hid_t[0:m, i, :], ps_s[0:m, i % 3, S:2 * S],
                                                   sgu[0:m, 1, i:i + 1], gate[0:m, i % 2, :],
                                                   ALU.mult, ALU.mult).then_inc(hid_done, 1)

            def result(b):
                dve.wait_ge(dn_ps, b * TB + TB)
                nc.vector.tensor_tensor(x1[:, bass.ds(b * TB, TB), :], ps_p[:, :, 0:HID],
                                        xs[:, bass.ds(b * TB, TB), :], ALU.add).then_inc(res_done, 1)

            def ffn(b, last):
                if not last:
                    gate_z(b + 1)
                hidden(b)
                if not last:
                    norm_x2(b + 1)
                result(b)

            gate_z(0)
            norm_x2(0)
            add_attention(LAST)
            x1_stats(LAST, B)
            x1_nmr(LAST, B, 3)
            ffn(0, False)
            with dve.Fori(1, LAST) as b:
                ffn(b, False)
            ffn(LAST, True)

        @block.tensor
        def _(pe):
            pe.sem_inc(wo_done, 1)
            pe.wait_ge(consts, 9)

            def transpose_x(i):
                pe.wait_ge(ln_x, TB * (i + 1))
                if i >= 2:
                    pe.wait_ge(xt_sb, i - 1)
                for k in range(KT):
                    for t in range(TB):
                        last = nc.tensor.transpose(ps_r[:, i % 2, k * S + t * P:k * S + (t + 1) * P],
                                                   x1[:, i * TB + t, k * P:(k + 1) * P], ident[:])
                last.then_inc(xt_ps, 1)

            pe.wait_ge(ctx_in, 32)
            for i in range(2 * EB):
                e, h = divmod(i, 2)
                dst = ps_s[:, i, :] if i < 3 else ps_o[:]
                nc.tensor.matmul(dst, inproj[:, e * P:(e + 1) * P], ctxs[:, h * 512:(h + 1) * 512],
                                 start=True, stop=True).then_inc(inp_ps, 1)
            for i in range(B):
                transpose_x(i)

            def project(b, g):
                u = mulof(b, KVH) + g
                gg = g % KVH
                if gg == 0:
                    pe.wait_ge(xt_ready, b + 1 + g // KVH)
                for t in range(TB):
                    if not (isinstance(b, int) and 8 * b + g < 1):
                        pe.wait_ge(rope_mul, u * 4 - 2 * (TB - 1 - t))
                        pe.wait_ge(v_copied, u * 2 - (TB - 1 - t))
                    for k in range(KT):
                        last = nc.tensor.matmul(ps_p[:, t, 0:GC], xt[:, k, t * P:(t + 1) * P],
                                                wqkv[:, k, gg, :], start=(k == 0), stop=(k == KT - 1))
                    last.then_inc(proj_done, 1)

            def transpose_qk(b, g):
                u = mulof(b, KVH) + g
                slot = g - 2
                for t in range(TB):
                    pe.wait_ge(rope_add, u * 4 + 2 * (t + 1))
                    bank = (5 * slot + 3 + t) % 2
                    if t == 0:
                        if isinstance(b, int) and b == 0 and g == 0:
                            pe.wait_ge(xt_sb, B)
                        else:
                            pe.wait_ge(qkt_copied, u * 2)
                        if slot >= 0:
                            pe.wait_ge(pt_dve, u)
                    elif slot >= 0:
                        pe.wait_ge(pt_act, u * 2 - 1)
                    for k in range(3):
                        last = nc.tensor.transpose(ps_r[:, bank, k * P:(k + 1) * P],
                                                   qkn[:, g % 2, t, k * P:(k + 1) * P], ident[:])
                    last.then_inc(qkt_done, 1)

            def scores(b, g):
                u = mulof(b, KVH) + g
                r = g % 2
                pe.wait_ge(qkt_copied, u * 2 + 2)
                first = isinstance(b, int) and 8 * b + g < 1

                def dot(bank, col, h, t, keys, start=False):
                    lo = (h % 2) * HD
                    return nc.tensor.matmul(ps_s[:, bank, col:col + keys],
                                            qkt[lo:lo + HD, r, h // 2, t * P:(t + 1) * P],
                                            qkt[lo:lo + HD, r, 2, 0:keys], start=start, stop=False)

                def mask(bank):
                    if bank == 0:
                        o, m = ps_s[:, 0, :], mask_diag[:]
                    else:
                        o = ps_s[:, bank, :].rearrange("p (h t k) -> p h t k", h=2, t=TB)[:, :, 1, :]
                        m = mask_diag[:, 0:2 * P].rearrange("p (h k) -> p h k", h=2)
                    nc.tensor.matmul(o, ident_b[:], m, start=False, stop=True).then_inc(score_done, 1)

                if first:
                    pe.wait_ge(inp_sb, 2 * EB)
                else:
                    pe.wait_ge(exp_done, u * 8)
                dot(0, 0, 0, 0, P, start=True)
                dot(2, 0, 1, 1, S, start=True)
                dot(0, 2 * P, 2, 0, P).then_inc(even_done, 1)
                dot(2, S, 3, 1, S)
                mask(2)
                dot(1, 0, 0, 1, S, start=True)
                pe.wait_ge(even_done, u + 1)
                dot(0, P, 1, 0, P)
                dot(1, S, 2, 1, S)
                mask(1)
                dot(0, 3 * P, 3, 0, P)
                mask(0)

            place = [0, 2, 1, 3]

            def transpose_p(b, g, qk_before):
                u = mulof(b, KVH) + g
                r = g % 2
                pe.wait_ge(norm_done, u * 8 + 9)
                for fill in range(3):
                    bank = (5 * g + fill) % 2
                    if fill == 2:
                        pe.wait_ge(pt_act, u * 2 + 2)
                    elif qk_before:
                        pe.wait_ge(qkt_copied, u * 2 + 3 + fill)
                    elif fill == 0:
                        pe.wait_ge(pt_dve, u + 1)
                    else:
                        pe.wait_ge(pt_act, u * 2 + 1)
                    for k in range(4):
                        if fill < 2:
                            h = 2 * fill + k // 2
                            src = prob0[:, r, h, :] if k % 2 == 0 else prob1[:, r, place[h], 0:P]
                        else:
                            src = prob1[:, r, place[k], P:S]
                        last = nc.tensor.transpose(ps_r[:, bank, k * P:(k + 1) * P], src, ident[:])
                    last.then_inc(pt_done, 1)

            def values(b, g):
                u = mulof(b, KVH) + g
                if not (isinstance(b, int) and 8 * b + g < 1):
                    pe.wait_ge(attn_copied, u + 1)
                    if g == 0:
                        pe.wait_ge(x1_done, b + 1)
                pe.wait_ge(v_copied, u * 2 + 2)
                pe.wait_ge(pt_act, u * 2 + 3)
                pe.wait_ge(pt_dve, u + 2)
                for pair in range(GRP // 2):
                    for part in range(2):
                        for odd in range(2):
                            o = ps_o[odd * HD:(odd + 1) * HD, :]
                            if part == 0:
                                last = nc.tensor.matmul(o[:, pair * S:(pair + 1) * S], vv[:, g % 4, 0, :],
                                                        pt[:, pair, odd * S:(odd + 1) * S], start=True, stop=False)
                            else:
                                h = 2 * pair + odd
                                last = nc.tensor.matmul(o[:, pair * S + P:(pair + 1) * S], vv[:, g % 4, 1, :],
                                                        pt[:, 2, h * P:(h + 1) * P], start=False, stop=True)
                last.then_inc(pv_done, 1)

            def out_project(b):
                pe.wait_ge(wo_in, 16)
                pe.wait_ge(attn_copied, b * 8 + 9)
                for t in range(TB):
                    for k in range(H // 2):
                        last = nc.tensor.matmul(ps_o[:, t * HID:(t + 1) * HID], attn_t[:, k, t * P:(t + 1) * P],
                                                wo[:, k, :], start=(k == 0), stop=(k == H // 2 - 1))
                last.then_inc(wo_done, 1)

            pe.wait_ge(wqkv_in, 16)
            project(0, 0)
            project(0, 1)
            transpose_qk(0, 0)
            transpose_qk(0, 1)
            pe.wait_ge(ssm_in, 32)
            pe.wait_ge(u_done, EB)
            pe.wait_ge(rope_mul, 8)
            pe.wait_ge(v_copied, 4)
            for h in range(2):
                for e in range(EB):
                    last = nc.tensor.matmul(ps_p[0:XR, h, :], xproj[:, e, :], u_s[:, e, h * 512:(h + 1) * 512],
                                            start=(e == 0), stop=(e == EB - 1))
                last.then_inc(xdbl_ps, 1)
            scores(0, 0)
            pe.wait_ge(xdbl_sb, 2)
            pe.wait_ge(qkt_copied, 4)
            for e in range(EB):
                for h in range(2):
                    if e == 1:
                        pe.wait_ge(dt_v, h + 1)
                    nc.tensor.matmul(ps_r[:, h, :], dtproj[:, e * P:(e + 1) * P], xdbl[0:DR, h * 512:(h + 1) * 512],
                                     start=True, stop=True).then_inc(dt_ps, 1)
            pe.wait_ge(wqkv_in2, 16)
            pe.wait_ge(dt_v, 2 * EB)
            project(0, 2)

            def batch(b, first, last):
                for g in range(KVH):
                    if not (last and g + 1 >= KVH):
                        scores(b, g + 1)
                    if g == 0 and not first:
                        out_project(b - 1)
                    transpose_p(b, g, not (last and g + 1 >= KVH))
                    if not (last and g + 3 >= KVH):
                        project(b, g + 3)
                    if not (last and g + 2 >= KVH):
                        transpose_qk(b, g + 2)
                    values(b, g)
                if last:
                    transpose_gz(0)
                    out_project(b)

            def transpose_gz(b):
                pe.wait_ge(gz_done, b + 1)
                if isinstance(b, int) and b == 0:
                    pe.wait_ge(pt_dve, 1 + UNITS)
                    pe.wait_ge(pt_act, 1 + 2 * UNITS)
                else:
                    pe.wait_ge(x2_done, b)
                for lt in range(TB):
                    for et in range(EB):
                        last = nc.tensor.transpose(ps_r[:, 0, lt * HID + et * P:lt * HID + (et + 1) * P],
                                                   gz[:, et, lt * P:(lt + 1) * P], ident[:])
                last.then_inc(gt_ps, 1)

            def transpose_x2(b):
                pe.wait_ge(xh2_done, b * TB + TB)
                if not (isinstance(b, int) and b == 0):
                    pe.wait_ge(x2t_sb, b)
                for k in range(KT):
                    for t in range(TB):
                        last = nc.tensor.transpose(ps_r[:, 1, k * S + t * P:k * S + (t + 1) * P],
                                                   xh2[:, t, k * P:(k + 1) * P], ident[:])
                last.then_inc(x2t_ps, 1)

            def gate_up(b):
                pe.wait_ge(x2t_sb, b + 1)
                for i in range(HT):
                    m = HP[i]
                    if not (isinstance(b, int) and b == 0 and i < 3):
                        pe.wait_ge(hid_done, b * HT + i - 2)
                    for w in range(2):
                        for k in range(KT):
                            last = nc.tensor.matmul(ps_s[0:m, i % 3, w * S:(w + 1) * S],
                                                    wgu[:, w, k, i * P:i * P + m], xh2_t[:, k, :],
                                                    start=(k == 0), stop=(k == KT - 1))
                    last.then_inc(gu_ps, 1)

            def down(b):
                pe.wait_ge(hid_done, b * HT + HT)
                if not (isinstance(b, int) and b == 0):
                    pe.wait_ge(res_done, b)
                for t in range(TB):
                    for i in range(HT):
                        m = HP[i]
                        last = nc.tensor.matmul(ps_p[:, t, 0:HID], hid_t[0:m, i, t * P:(t + 1) * P],
                                                wdn[0:m, i, :], start=(i == 0), stop=(i == HT - 1))
                    last.then_inc(dn_ps, 1)

            def ffn(b, last):
                if not last:
                    transpose_gz(b + 1)
                gate_up(b)
                down(b)
                if not last:
                    transpose_x2(b + 1)

            batch(0, True, False)
            with pe.Fori(1, LAST) as b:
                batch(b, False, False)
            batch(LAST, False, True)

            pe.wait_ge(wq_done, 1 + HT)
            transpose_x2(0)
            ffn(0, False)
            with pe.Fori(1, LAST) as b:
                ffn(b, False)
            ffn(LAST, True)


def kernel(x, ctx_1024, L0_attn_Wq, L0_attn_Wk, L0_attn_Wv, L0_attn_Wo, L0_xattn_in_proj_w, L0_xattn_conv_w,
           L0_xattn_conv_b, L0_xattn_x_proj_w, L0_xattn_dt_proj_w, L0_xattn_dt_proj_b, L0_xattn_A_log,
           L0_xattn_D, L0_ffn_wq_gate, L0_ffn_s_gate, L0_ffn_wq_up, L0_ffn_s_up, L0_ffn_wq_down,
           L0_ffn_s_down):
    import concourse.bacc as bacc
    from concourse.bass_utils import run_bass_kernel_spmd

    inv = (1.0 / (10000.0 ** (np.arange(0, HD, 2, dtype=np.float32) / np.float32(HD)))).astype(np.float32)
    freq = np.arange(S, dtype=np.float32)[:, None] * inv[None, :]
    cos, sin = np.cos(freq), np.sin(freq)
    scale = np.repeat(np.array([HD ** -0.5] * GRP + [1.0], np.float32), HD)
    cos_t = (np.tile(cos, (1, 2 * (GRP + 1))) * scale).astype(np.float32)
    sin_t = (np.tile(np.concatenate([-sin, sin], 1), (1, GRP + 1)) * scale).astype(np.float32)

    rows = [np.asarray(w).reshape(KVH, -1, HID) for w in (L0_attn_Wq, L0_attn_Wk, L0_attn_Wv)]
    column = lambda v: np.asarray(v).reshape(DI, -1)
    arrays = {
        "x": np.asarray(x).reshape(L, HID),
        "ctx_t": np.asarray(ctx_1024).reshape(L, DM).T,
        "wqkv_t": np.concatenate(rows, 1).transpose(2, 0, 1),
        "wo_t": np.asarray(L0_attn_Wo).T,
        "cos_t": cos_t,
        "sin_t": sin_t,
        "inproj_t": np.asarray(L0_xattn_in_proj_w).T,
        "ssm_par": np.concatenate([column(v) for v in (L0_xattn_conv_w, L0_xattn_conv_b, L0_xattn_dt_proj_b,
                                                       L0_xattn_D, L0_xattn_A_log)], 1),
        "xproj_t": np.asarray(L0_xattn_x_proj_w).T,
        "dtproj_t": np.asarray(L0_xattn_dt_proj_w).T,
        "wgate_t": np.asarray(L0_ffn_wq_gate).T,
        "wup_t": np.asarray(L0_ffn_wq_up).T,
        "wdown_t": np.asarray(L0_ffn_wq_down).T,
        "s_gate": np.asarray(L0_ffn_s_gate),
        "s_up": np.asarray(L0_ffn_s_up),
        "s_down": np.asarray(L0_ffn_s_down),
    }
    arrays = {k: np.ascontiguousarray(v) for k, v in arrays.items()}
    nc = bacc.Bacc("TRN2", target_bir_lowering=False, num_devices=1)
    args = [nc.dram_tensor(k, v.shape, mybir.dt.from_np(v.dtype), kind="ExternalInput").ap()
            for k, v in arrays.items()]
    bc_scratch = nc.dram_tensor("bc_scratch", (2 * NS, L), F32, kind="Internal").ap()
    out = nc.dram_tensor("out", (B, S, HID), F32, kind="ExternalOutput").ap()
    decoder_layer(nc, *args, bc_scratch, out)
    r = run_bass_kernel_spmd(nc, [arrays], core_ids=[0])
    return r.results[0]["out"]
```

```python
from contextlib import ExitStack

import numpy as np

import concourse.bass as bass
from concourse import mybir

F32 = mybir.dt.float32
BF16 = mybir.dt.bfloat16
F16 = mybir.dt.float16
I32 = mybir.dt.int32
ALU = mybir.AluOpType
ACT = mybir.ActivationFunctionType
AX = mybir.AxisListType

P = 128
B, S, HID = 4, 256, 256
H, KVH, HD = 32, 8, 64
GRP = H // KVH
TB = S // P
KT = HID // P
UNITS = B * KVH
ROT = (GRP + 1) * HD
QKC = ROT + HD
GC = (GRP + 2) * HD
NS = 16
DM = 128
DI = 256
EB = DI // P
DC = 4
DR = 8
XR = DR + 2 * NS
L = B * S
HF = 704
HT = -(-HF // P)
HP = [min(P, HF - P * i) for i in range(HT)]
EPS = 1e-5
ZERO_POINT = 128.0
MASKED = -3.0e38
FIRST_SCANS = [0, 0, 0, 0, 1, 1, 2, 2]
LAG = KVH - sum(FIRST_SCANS)
LAST_SCANS = [1, 1, 1, 1, 1, 2, 1, 2]
NPAR = DC + 3 + NS


def decoder_layer(nc, x, ctx_t, wqkv_t, wo_t, cos_t, sin_t, inproj_t, ssm_par, xproj_t, dtproj_t,
                  wgate_t, wup_t, wdown_t, s_gate, s_up, s_down, bc_scratch, out):
    ctx = ExitStack()
    with ctx:
        def sb(name, shape, dt=F32):
            return ctx.enter_context(nc.sbuf_tensor(name, shape, dt))

        def sem(name):
            return ctx.enter_context(nc.semaphore(name))

        wqkv = sb("wqkv", [P, KT, KVH, GC])
        wo = sb("wo", [P, H // 2, HID])
        wgu_i = sb("wgu_i", [P, KT, HF], I32)
        wgu = sb("wgu", [P, 2, KT, HF], F16)
        wdn_i = sb("wdn_i", [P, HT, HID], I32)
        wdn = wdn_i[:].bitcast(F32)
        sgu = sb("sgu", [P, 2, HT])
        sdn = sb("sdn", [P, HID])
        cos_s = sb("cos_s", [P, TB, ROT])
        sin_s = sb("sin_s", [P, TB, ROT])
        xs = sb("xs", [P, B * TB, HID])
        x1 = sb("x1", [P, B * TB, HID])
        xt_all = sb("xt_all", [P, KT, L])
        xt = sb("xt", [P, KT, S])
        stats = sb("stats", [P, B * TB, 6])
        mv = sb("mv", [P, B * TB, 2])
        rstd = sb("rstd", [P, B * TB])
        mv1 = sb("mv1", [P, B * TB, 2])
        rstd1 = sb("rstd1", [P, B * TB])
        nmr1 = sb("nmr1", [P, B * TB])
        mv2 = sb("mv2", [P, TB, 2])
        rstd2 = sb("rstd2", [P, TB])
        half = sb("half", [P, B * TB])
        eps = sb("eps", [P, TB])
        ident = sb("ident", [P, P])
        ident_b = sb("ident_b", [P, P], BF16)
        mask_diag = sb("mask_diag", [P, GRP * P], BF16)
        ropec = sb("ropec", [P, TB, ROT])
        ropes = sb("ropes", [P, TB, ROT])
        qkn = sb("qkn", [P, 2, TB, QKC])
        qkt = sb("qkt", [P, 2, 3, S])
        vv = sb("vv", [P, 4, TB, HD])
        nmax = sb("nmax", [P, 2, 2 * GRP])
        rsum = sb("rsum", [P, 2, 2 * GRP])
        rinv = sb("rinv", [P, 2, 2 * GRP])
        prob0 = sb("prob0", [P, 2, GRP, P])
        prob1 = sb("prob1", [P, 2, GRP, S])
        pt = sb("pt", [P, 3, 4 * P])
        attn_t = sb("attn_t", [P, H // 2, S])
        par = sb("par", [P, EB, NPAR])
        a_neg = sb("a_neg", [P, EB, NS])
        a_exp = sb("a_exp", [P, EB, NS])
        inproj = sb("inproj", [P, DI])
        xproj = sb("xproj", [P, EB, XR])
        dtproj = sb("dtproj", [DR, DI])
        delta = sb("delta", [P, EB, L])
        du = sb("du", [P, EB, L])
        y = sb("y", [P, EB, L])
        decay = sb("decay", [P, 2, L])
        state = sb("state", [P, 2, L])
        bc = sb("bc", [P, 2, 2, L])
        ctxs = bc[:, 0, 0, :]
        u_s = bc[:, 1, :, :]
        conv_in = attn_t[:].rearrange("p a s -> p (a s)")[:, 0:EB * B * (S + DC - 1)].rearrange(
            "p (e b s) -> p e b s", e=EB, b=B)
        xdbl = attn_t[:].rearrange("p a s -> p (a s)")[0:XR, 3 * L:4 * L]
        flat_n = qkn[:].rearrange("p r t n -> p (r t n)")
        flat_t = qkt[:].rearrange("p r k s -> p (r k s)")
        sz = flat_n[:, 0:TB * HID].rearrange("p (t n) -> p t n", t=TB)
        gz = flat_n[:, TB * HID:2 * TB * HID].rearrange("p (t n) -> p t n", t=TB)
        xh2 = flat_t[:, 0:TB * HID].rearrange("p (t n) -> p t n", t=TB)
        xh2_t = flat_t[:, TB * HID:2 * TB * HID].bitcast(F16).rearrange("p (c k n) -> p c k n", c=2, k=KT)
        gate = ropec[:].rearrange("p t n -> p (t n)")[:, 0:2 * S].rearrange("p (r s) -> p r s", r=2)
        hid_t = prob1[:].rearrange("p a b s -> p (a b s)")[:, 0:HT * S].rearrange(
            "p (h s) -> p h s", h=HT)

        ps_s = ctx.enter_context(nc.psum_tensor("ps_s", [P, 3, 512], F32))
        ps_r = ctx.enter_context(nc.psum_tensor("ps_r", [P, 2, 512], F32))
        ps_p = ctx.enter_context(nc.psum_tensor("ps_p", [P, 2, 512], F32))
        ps_o = ctx.enter_context(nc.psum_tensor("ps_o", [P, 512], F32))

        x_in, ssm_in, wqkv_in, tab_in, wo_in, ffn_in = (
            sem(n) for n in ("x_in", "ssm_in", "wqkv_in", "tab_in", "wo_in", "ffn_in"))
        up_in, wqkv_in2, ctx_in, par_in = (sem(n) for n in ("up_in", "wqkv_in2", "ctx_in", "par_in"))
        act_warm = sem("act_warm")
        bc_out, bc_in0, bc_in1, out_done = (sem(n) for n in ("bc_out", "bc_in0", "bc_in1", "out_done"))
        bc_in = [bc_in0, bc_in1]
        consts = sem("consts")
        ln_stat, ln_rstd, ln_x = sem("ln_stat"), sem("ln_rstd"), sem("ln_x")
        xt_ps, xt_sb, xt_ready = sem("xt_ps"), sem("xt_sb"), sem("xt_ready")
        v_chain, p_chain = sem("v_chain"), sem("p_chain")
        inp_ps, inp_sb, u_done = sem("inp_ps"), sem("inp_sb"), sem("u_done")
        conv_done0, conv_done1, conv_done2 = sem("conv_done0"), sem("conv_done1"), sem("conv_done2")
        xdbl_ps, xdbl_sb, dt_ps, dt_v = sem("xdbl_ps"), sem("xdbl_sb"), sem("dt_ps"), sem("dt_v")
        sp_e, sp_w, sp_l, a_done = sem("sp_e"), sem("sp_w"), sem("sp_l"), sem("a_done")
        sp_c = sem("sp_c")
        ssm_ready = sem("ssm_ready")
        proj_done = sem("proj_done")
        qkt_done = sem("qkt_done")
        score_done = sem("score_done")
        even_done = sem("even_done")
        pt_done = sem("pt_done")
        pv_done = sem("pv_done")
        wo_done = sem("wo_done")
        rope_mul = sem("rope_mul")
        v_copied = sem("v_copied")
        nmax_done = sem("nmax_done")
        rinv_done = sem("rinv_done")
        pt_1 = sem("pt_1")
        pt_act = sem("pt_act")
        qkt_copied = sem("qkt_copied")
        exp_done = sem("exp_done")
        attn_copied = sem("attn_copied")
        rope_add = sem("rope_add")
        norm_done = sem("norm_done")
        decay_done = sem("decay_done")
        decay_free = sem("decay_free")
        drive_done = sem("drive_done")
        hc_done = sem("hc_done")
        state_free = sem("state_free")
        x1_done = sem("x1_done")
        st1_done = sem("st1_done")
        r1_done = sem("r1_done")
        sz_done, gz_done = sem("sz_done"), sem("gz_done")
        gt_ps, x2_done, st2_done, r2_done = sem("gt_ps"), sem("x2_done"), sem("st2_done"), sem("r2_done")
        xh2_done, x2t_ps, x2t_sb = sem("xh2_done"), sem("x2t_ps"), sem("x2t_sb")
        bn2_done = sem("bn2_done")
        gu_ps, gate_done, hid_done = sem("gu_ps"), sem("gate_done"), sem("hid_done")
        dn_ps, res_done = sem("dn_ps"), sem("res_done")
        wq_done = sem("wq_done")
        x2lo_done = sem("x2lo_done")

        LAST = B - 1

        def scans(b, g):
            if g < 0:
                return [(b, g - LAG)]
            if not isinstance(b, int):
                return [(b, g - LAG)]
            counts, at = (FIRST_SCANS, 0) if b == 0 else (LAST_SCANS, -LAG)
            at += sum(counts[:g])
            return [(b, at + i) for i in range(counts[g])]

        mulof = lambda v, k: k * v

        block = ctx.enter_context(nc.Block())

        @block.sync
        def _(sp):
            sp.dma_start(xs[:], x.rearrange("(t p) n -> p t n", p=P)).then_inc(x_in, 16)
            sp.dma_start(xproj[:], xproj_t.rearrange("(e p) n -> p e n", p=P)).then_inc(ssm_in, 16)
            sp.dma_start(dtproj[:], dtproj_t).then_inc(ssm_in, 16)
            w = wqkv_t.rearrange("(k p) g n -> p k g n", p=P)
            sp.dma_start(wqkv[:, :, 0:2, :], w[:, :, 0:2, :]).then_inc(wqkv_in, 16)
            sp.dma_start(cos_s[:], cos_t.rearrange("(t p) n -> p t n", p=P)).then_inc(tab_in, 16)
            sp.dma_start(sin_s[:], sin_t.rearrange("(t p) n -> p t n", p=P)).then_inc(tab_in, 16)
            sp.dma_start(wqkv[:, :, 2:KVH, :], w[:, :, 2:KVH, :]).then_inc(wqkv_in2, 16)
            sp.wait_ge(xdbl_sb, 2)
            sp.dma_start(bc_scratch, xdbl[DR:XR, :]).then_inc(bc_out, 16)
            sp.wait_ge(bc_out, 16)

            def load_bc(n):
                for c in range(2):
                    sp.dma_start(bc[:, n, c, :], bc_scratch[c * NS + n:c * NS + n + 1, :].to_broadcast([P, L])
                                 ).then_inc(bc_in[n], 16)

            load_bc(0)
            sp.dma_start(wo[:], wo_t.rearrange("(k p) n -> p k n", p=P)).then_inc(wo_in, 16)
            sp.dma_start(wgu_i[:], wgate_t.rearrange("(k p) n -> p k n", p=P)).then_inc(ffn_in, 16)
            full = P * (HT - 1)
            sp.dma_start(wdn_i[:, 0:HT - 1, :], wdown_t[0:full, :].rearrange("(k p) n -> p k n", p=P)
                         ).then_inc(ffn_in, 16)
            sp.dma_start(wdn_i[0:HP[-1], HT - 1, :], wdown_t[full:HF, :]).then_inc(ffn_in, 16)
            for i, s in enumerate((s_gate, s_up)):
                with nc.allow_non_contiguous_dma(reason="704 scales, once"):
                    sp.dma_start(sgu[:, i, 0:HT - 1], s[0:full].rearrange("(k p) -> p k", p=P)
                                 ).then_inc(ffn_in, 16)
                    sp.dma_start(sgu[0:HP[-1], i, HT - 1:HT], s[full:HF].rearrange("(p k) -> p k", k=1)
                                 ).then_inc(ffn_in, 16)
            sp.dma_start(sdn[:], s_down.rearrange("(a n) -> a n", a=1).to_broadcast([P, HID])
                         ).then_inc(ffn_in, 16)
            sp.wait_ge(ssm_ready, 5)
            load_bc(1)
            sp.wait_ge(wq_done, 1)
            sp.dma_start(wgu_i[:], wup_t.rearrange("(k p) n -> p k n", p=P)).then_inc(up_in, 16)
            with sp.Fori(0, NS // 2 - 1) as j:
                for k in range(2):
                    sp.wait_ge(hc_done, j * 4 + 2 * k + 2)
                    for c in range(2):
                        sp.dma_start(bc[:, k, c, :],
                                     bc_scratch[bass.ds(j * 2 + (c * NS + k + 2), 1), :].to_broadcast([P, L])
                                     ).then_inc(bc_in[k], 16)
            with sp.Fori(0, B) as b:
                sp.wait_ge(res_done, b + 1)
                sp.dma_start(out[bass.ds(b, 1), :, :].rearrange("b (t p) n -> p (b t) n", p=P),
                             x1[:, bass.ds(b * TB, TB), :]).then_inc(out_done, 16)
            sp.wait_ge(out_done, 16 * B)

        @block.gpsimd
        def _(pool):
            pool.sem_inc(norm_done, 1)
            nc.gpsimd.memset(half[:], -0.5).then_inc(consts, 1)
            nc.gpsimd.memset(eps[:], EPS).then_inc(consts, 1)
            nc.gpsimd.memset(ident[:], 0.0).then_inc(consts, 1)
            nc.gpsimd.memset(ident_b[:], 0.0).then_inc(consts, 1)
            nc.gpsimd.memset(mask_diag[:], 0.0).then_inc(consts, 1)
            nc.gpsimd.memset(conv_in[:, :, :, 0:DC - 1], 0.0).then_inc(consts, 1)
            pool.wait_ge(consts, 6)
            for m in (ident, ident_b):
                nc.gpsimd.affine_select(out=m[:], in_=m[:], compare_op=ALU.not_equal, fill=1.0, base=0,
                                        pattern=[[-1, P]], channel_multiplier=1).then_inc(consts, 1)
            m0 = mask_diag[:].rearrange("p (h k) -> p h k", h=GRP)
            nc.gpsimd.affine_select(out=m0, in_=m0, compare_op=ALU.is_ge, fill=MASKED, base=0,
                                    pattern=[[0, GRP], [-1, P]], channel_multiplier=1).then_inc(consts, 1)
            pool.wait_ge(act_warm, 1)
            pool.wait_ge(ln_stat, B * TB)
            nc.gpsimd.tensor_scalar(rstd[:], mv[:, :, 1], EPS, 1.0, ALU.add, ALU.mult).then_inc(p_chain, 1)
            pool.wait_ge(p_chain, 1)
            nc.gpsimd.tensor_tensor(rstd[:], rstd[:], half[:], ALU.pow).then_inc(ln_rstd, 1)
            half_of = lambda v: v.rearrange("p (b s) -> p b s", b=B)[:, 0:B // 2, :]
            acc, tap = half_of(du[:, 1, :]), half_of(y[:, 1, :])
            pool.wait_ge(par_in, 16)
            pool.wait_ge(inp_sb, 2 * EB)
            nc.gpsimd.tensor_scalar(acc, conv_in[:, 1, 0:B // 2, 0:S], par[:, 1, 0:1], par[:, 1, DC:DC + 1],
                                    ALU.mult, ALU.add).then_inc(conv_done1, 1)
            for j in range(1, DC):
                if j > 1:
                    pool.wait_ge(conv_done1, 2 * j - 1)
                nc.gpsimd.tensor_scalar(tap, conv_in[:, 1, 0:B // 2, j:j + S], par[:, 1, j:j + 1], 1.0,
                                        ALU.mult, ALU.mult).then_inc(conv_done1, 1)
                pool.wait_ge(conv_done1, 2 * j)
                nc.gpsimd.tensor_tensor(acc, acc, tap, ALU.add).then_inc(conv_done1, 1)
            pool.sem_inc(state_free, 2)

            def add_rope(b, g):
                u = mulof(b, KVH) + g
                for t in range(TB):
                    pool.wait_ge(rope_mul, u * 4 + 2 * (t + 1))
                    if t == 0 and not (isinstance(b, int) and 8 * b + g < 2):
                        pool.wait_ge(qkt_done, u * 2 - 2)
                    o = qkn[:, g % 2, t, :]
                    nc.gpsimd.tensor_tensor(o[:, 0:ROT], ropec[:, t, :], ropes[:, t, :], ALU.add
                                            ).then_inc(rope_add, 1)
                    nc.gpsimd.tensor_tensor(o[:, ROT:QKC], ropec[:, t, ROT - HD:], ropes[:, t, ROT - HD:],
                                            ALU.add).then_inc(rope_add, 1)

            def normalise(b, g):
                u = mulof(b, KVH) + g
                pool.wait_ge(consts, 9)
                pool.wait_ge(rinv_done, u + 1)
                for h in range(GRP):
                    nc.gpsimd.tensor_scalar(prob0[:, g % 2, h, :], prob0[:, g % 2, h, :],
                                            rinv[:, g % 2, h:h + 1], 1.0, ALU.mult, ALU.mult
                                            ).then_inc(norm_done, 1)
                for h in range(GRP):
                    nc.gpsimd.tensor_scalar(prob1[:, g % 2, h, :], prob1[:, g % 2, h, :],
                                            rinv[:, g % 2, GRP + h:GRP + h + 1], 1.0, ALU.mult, ALU.mult
                                            ).then_inc(norm_done, 1)

            def add_y(b, g):
                u = mulof(b, KVH) + g
                pool.wait_ge(hc_done, u + 1)
                pool.wait_ge(state_free, u + 1)
                nc.gpsimd.tensor_tensor(y[:, g % 2, :], y[:, g % 2, :], state[:, g % 2, :], ALU.add
                                        ).then_inc(state_free, 1)

            add_rope(0, 0)
            add_rope(0, 1)
            normalise(0, 0)

            def x1_rstd(lo, hi, step):
                r = rstd1[:, lo * TB:hi * TB]
                pool.wait_ge(st1_done, hi * TB)
                nc.gpsimd.tensor_scalar(r, mv1[:, lo * TB:hi * TB, 1], EPS, 1.0, ALU.add, ALU.mult
                                        ).then_inc(p_chain, 1)
                pool.wait_ge(p_chain, step)
                nc.gpsimd.tensor_tensor(r, r, half[:, lo * TB:hi * TB], ALU.pow).then_inc(r1_done, 1)

            def batch(b, first, last):
                for g in range(KVH):
                    if not (last and g + 2 >= KVH):
                        add_rope(b, g + 2)
                    if not (first and g == 0):
                        for v in scans(b, g - 1):
                            add_y(*v)
                    if not (last and g + 1 >= KVH):
                        normalise(b, g + 1)
                    if last and g == 2:
                        x1_rstd(0, LAST, 2)
                if first:
                    for v in scans(b, KVH - 1)[:-1]:
                        add_y(*v)

            batch(0, True, False)
            with pool.Fori(1, LAST) as b:
                batch(b, False, False)
            batch(LAST, False, True)

            for v in scans(LAST, KVH - 1):
                add_y(*v)

            def ffn_rstd(b):
                pool.wait_ge(st2_done, mulof(b, TB) + TB)
                nc.gpsimd.tensor_tensor(rstd2[:], mv2[:, :, 1], eps[:], ALU.add).then_inc(p_chain, 1)
                pool.wait_ge(p_chain, b + (4 if not isinstance(b, int) else 3))
                nc.gpsimd.tensor_tensor(rstd2[:], rstd2[:], half[:, 0:TB], ALU.pow).then_inc(r2_done, 1)

            ffn_rstd(0)
            ffn_rstd(1)
            x1_rstd(LAST, B, 5)
            with pool.Fori(2, B) as b:
                ffn_rstd(b)

        @block.scalar
        def _(act):
            def copy_qkt(b, g):
                u = mulof(b, KVH) + g
                slot = g - 2
                for t in range(TB):
                    act.wait_ge(qkt_done, u * 2 + t + 1)
                    bank = (5 * slot + 3 + t) % 2
                    nc.scalar.activation(qkt[:, g % 2, :, t * P:(t + 1) * P],
                                         ps_r[:, bank, 0:3 * P].rearrange("p (k s) -> p k s", k=3), ACT.Copy
                                         ).then_inc(qkt_copied, 1)

            def exps(b, g, part):
                u = mulof(b, KVH) + g
                act.wait_ge(nmax_done, u * 3 + 3 - part)
                r = g % 2
                for k in range(GRP if part == 0 else 2):
                    if part == 0:
                        o, i, c = prob0[:, r, k, :], ps_s[:, 0, k * P:(k + 1) * P], k
                    else:
                        c = GRP + 2 * (part - 1) + k
                        o, i = prob1[:, r, c - GRP, :], ps_s[:, part, k * S:(k + 1) * S]
                    nc.scalar.activation(o, i, ACT.Exp, bias=nmax[:, r, c:c + 1],
                                         accum_out=rsum[:, r, c:c + 1]).then_inc(exp_done, 1)

            def copy_pt(b, g, fill):
                u = mulof(b, KVH) + g
                act.wait_ge(pt_done, u * 3 + fill + 1)
                nc.scalar.activation(pt[:, fill, :], ps_r[:, (5 * g + fill) % 2, :], ACT.Copy
                                     ).then_inc(pt_1 if fill == 1 else pt_act, 1)

            def copy_attn(b, g):
                u = mulof(b, KVH) + g
                act.wait_ge(pv_done, u + 1)
                if g == 0 and not (isinstance(b, int) and b == 0):
                    act.wait_ge(wo_done, b + 1)
                nc.scalar.activation(attn_t[:, 2 * g:2 * g + 2, :],
                                     ps_o[:].rearrange("p (k s) -> p k s", k=2), ACT.Copy
                                     ).then_inc(attn_copied, 1)

            def decays(b, g):
                u = mulof(b, KVH) + g
                n = b * (KVH // 2) + g // 2
                act.wait_ge(decay_free, u + 1)
                nc.scalar.activation(
                    decay[:, g % 2, :].rearrange("p (b s) -> p b s", b=B)[:, :, 1:],
                    delta[:, g % 2, :].rearrange("p (b s) -> p b s", b=B)[:, :, 1:],
                    ACT.Exp, scale=a_neg[:, g % 2, bass.ds(n, 1)]).then_inc(decay_done, 1)

            nc.scalar.dma_start(inproj[:], inproj_t).then_inc(ctx_in, 16)
            nc.scalar.dma_start(ctxs, ctx_t).then_inc(ctx_in, 16)
            nc.scalar.dma_start(par[:], ssm_par.rearrange("(e p) n -> p e n", p=P)).then_inc(par_in, 16)
            act.sem_inc(pt_act, 1)
            act.sem_inc(attn_copied, 1)
            act.wait_ge(consts, 2)
            nc.scalar.activation(rstd2[:], eps[:], ACT.Silu).then_inc(act_warm, 1)
            act.wait_ge(consts, 6)
            for i in range(2 * EB):
                e, h = divmod(i, 2)
                act.wait_ge(inp_ps, i + 1)
                src = ps_s[:, i, :] if i < 3 else ps_o[:]
                nc.scalar.activation(conv_in[:, e, 2 * h:2 * h + 2, DC - 1:],
                                     src.rearrange("p (b s) -> p b s", b=2), ACT.Copy).then_inc(inp_sb, 1)
            for i in range(B):
                act.wait_ge(xt_ps, i + 1)
                nc.scalar.activation(xt_all[:, :, i * S:(i + 1) * S],
                                     (ps_r[:, i % 2, :]).rearrange("p (k s) -> p k s", k=KT), ACT.Copy
                                     ).then_inc(xt_sb, 1)
            act.wait_ge(conv_done0, 2 * DC)
            nc.scalar.activation(u_s[:, 0, :], du[:, 0, :], ACT.Silu).then_inc(u_done, 1)
            copy_qkt(0, 0)
            copy_qkt(0, 1)
            act.wait_ge(conv_done1, 2 * DC - 1)
            act.wait_ge(conv_done2, DC)
            nc.scalar.activation(u_s[:, 1, :], du[:, 1, :], ACT.Silu).then_inc(u_done, 1)
            for i in range(2):
                act.wait_ge(xdbl_ps, i + 1)
                nc.scalar.activation(xdbl[:, i * 512:(i + 1) * 512], ps_p[0:XR, i, :], ACT.Copy
                                     ).then_inc(xdbl_sb, 1)
            for part in (2, 1, 0):
                exps(0, 0, part)
            nc.scalar.activation(a_exp[:], par[:, :, DC + 3:], ACT.Exp).then_inc(a_done, 1)

            def prepare_scan(g):
                for e in range(EB):
                    if g == 0:
                        act.wait_ge(dt_v, 2 * (e + 1))
                        nc.scalar.activation(decay[:, e, :], delta[:, e, :], ACT.Abs).then_inc(sp_e, 1)
                        act.wait_ge(sp_e, 2 * e + 1)
                        nc.scalar.activation(decay[:, e, :], decay[:, e, :], ACT.Exp, scale=-1.0
                                             ).then_inc(sp_e, 1)
                    elif g == 1:
                        act.wait_ge(sp_w, e + 1)
                        nc.scalar.activation(y[:, e, :], state[:, e, :], ACT.Ln).then_inc(sp_l, 1)
                if g == 3:
                    act.wait_ge(ssm_ready, 5)

            act.wait_ge(bc_out, 16)

            def batch(b, first, last):
                for g in range(KVH):
                    copy_pt(b, g, 0)
                    if last:
                        copy_pt(b, g, 1)
                    nxt = not (last and g + 1 >= KVH)
                    if nxt:
                        exps(b, g + 1, 2)
                        exps(b, g + 1, 1)
                    copy_pt(b, g, 2)
                    if nxt:
                        exps(b, g + 1, 0)
                    if not (last and g + 2 >= KVH):
                        copy_qkt(b, g + 2)
                    copy_attn(b, g)
                    if first and g < 4:
                        prepare_scan(g)
                    if last or first and g + 1 < KVH:
                        for v in scans(b, g + 1) if g + 1 < KVH else []:
                            decays(*v)
                    else:
                        decays(b, g + 1 - LAG)
                    if last and g == KVH - 2:
                        act.wait_ge(r1_done, 2)
                        silu_z(0)

            def silu_z(b):
                if not (isinstance(b, int) and b == 0):
                    act.wait_ge(gz_done, b)
                for t in range(TB):
                    nc.scalar.activation(sz[:, t, :], x1[:, bass.ds(b * TB + t, 1), :], ACT.Silu,
                                         bias=nmr1[:, bass.ds(b * TB + t, 1)],
                                         scale=rstd1[:, bass.ds(b * TB + t, 1)]).then_inc(sz_done, 1)

            def copy_x2t(b):
                act.wait_ge(x2t_ps, b + 1)
                nc.scalar.activation(xh2_t[:, 0, :, :], ps_r[:, 1, :].rearrange("p (k s) -> p k s", k=KT),
                                     ACT.Copy).then_inc(x2t_sb, 1)

            def gates(b):
                for i in range(HT):
                    act.wait_ge(gu_ps, b * HT + i + 1)
                    if not (isinstance(b, int) and b == 0 and i < 2):
                        act.wait_ge(hid_done, b * HT + i - 1)
                    m = HP[i]
                    nc.scalar.activation(gate[0:m, i % 2, :], ps_s[0:m, i % 3, 0:S], ACT.Silu,
                                         scale=sgu[0:m, 0, i:i + 1]).then_inc(gate_done, 1)

            def ffn(b, last):
                if not last:
                    silu_z(b + 1)
                gates(b)
                if not last:
                    copy_x2t(b + 1)

            batch(0, True, False)
            with act.Fori(1, LAST) as b:
                batch(b, False, False)
            batch(LAST, False, True)

            copy_x2t(0)
            act.wait_ge(ffn_in, 16 * 8)
            ffn(0, False)
            act.wait_ge(r1_done, 4)
            with act.Fori(1, LAST) as b:
                ffn(b, False)
            ffn(LAST, True)

        @block.vector
        def _(dve):
            chain = [0]

            def then(ins):
                chain[0] += 1
                ins.then_inc(v_chain, 1)
                dve.wait_ge(v_chain, chain[0])

            dve.sem_inc(pt_1, 1)
            dve.sem_inc(x1_done, 1)
            dve.wait_ge(x_in, 16)
            for i in range(B * TB):
                nc.vector.bn_stats(stats[:, i, :], xs[:, i, :]).then_inc(v_chain, 1)
            chain[0] += B * TB
            dve.wait_ge(v_chain, chain[0])
            for i in range(B * TB):
                nc.vector.bn_aggr(mv[:, i, :], stats[:, i, :]).then_inc(ln_stat, 1)
            dve.wait_ge(ln_rstd, 1)
            dve.wait_ge(ln_stat, B * TB)
            for i in range(B * TB):
                nc.vector.tensor_scalar(x1[:, i, :], xs[:, i, :], mv[:, i, 0:1], rstd[:, i:i + 1],
                                        ALU.subtract, ALU.mult).then_inc(ln_x, 1)
            dve.wait_ge(xt_sb, 1)
            nc.vector.tensor_copy(xt[:], xt_all[:, :, 0:S]).then_inc(xt_ready, 1)

            def rope(b, g):
                u = mulof(b, KVH) + g
                for t in range(TB):
                    dve.wait_ge(proj_done, u * 2 + t + 1)
                    if not (isinstance(b, int) and 8 * b + g < 1):
                        dve.wait_ge(rope_add, u * 4 - 2 * (TB - 1 - t))
                    q = ps_p[:, t, 0:ROT]
                    nc.vector.tensor_tensor(ropec[:, t, :], q, cos_s[:, t, :], ALU.mult).then_inc(rope_mul, 1)
                    swapped = q.rearrange("p (h two d) -> p h two d", two=2, d=HD // 2)[:, :, ::-1, :]
                    nc.vector.tensor_tensor(
                        ropes[:, t, :].rearrange("p (h two d) -> p h two d", two=2, d=HD // 2), swapped,
                        sin_s[:, t, :].rearrange("p (h two d) -> p h two d", two=2, d=HD // 2),
                        ALU.mult).then_inc(rope_mul, 1)
                    nc.vector.tensor_copy(vv[:, g % 4, t, :], ps_p[:, t, ROT:GC]).then_inc(v_copied, 1)

            def negmax(b, g):
                u = mulof(b, KVH) + g
                for part in (2, 1, 0):
                    dve.wait_ge(score_done, u * 3 + 3 - part)
                    k, c = (GRP, 0) if part == 0 else (2, GRP + 2 * (part - 1))
                    nc.vector.tensor_reduce(nmax[:, g % 2, c:c + k],
                                            ps_s[:, part, :].rearrange("p (k s) -> p k s", k=k),
                                            AX.X, ALU.max, negate=True).then_inc(nmax_done, 1)

            def reciprocals(b, g):
                u = mulof(b, KVH) + g
                dve.wait_ge(exp_done, u * 8 + 8)
                if not (isinstance(b, int) and 8 * b + g < 2):
                    dve.wait_ge(norm_done, u * 8 - 7)
                nc.vector.reciprocal(rinv[:, g % 2, :], rsum[:, g % 2, :]).then_inc(rinv_done, 1)

            def convolve(e, batches, done, before=0):
                dve.wait_ge(par_in, 16)
                dve.wait_ge(inp_sb, 2 * (e + 1))
                acc = du[:, e, :].rearrange("p (b s) -> p b s", b=B)[:, batches, :]
                nc.vector.tensor_scalar(acc, conv_in[:, e, batches, 0:S], par[:, e, 0:1], par[:, e, DC:DC + 1],
                                        ALU.mult, ALU.add).then_inc(done, 1)
                for j in range(1, DC):
                    dve.wait_ge(done, before + j)
                    nc.vector.scalar_tensor_tensor(acc, conv_in[:, e, batches, j:j + S], par[:, e, j:j + 1],
                                                   acc, ALU.mult, ALU.add).then_inc(done, 1)

            convolve(0, slice(0, B // 2), conv_done0)
            dve.wait_ge(tab_in, 32)
            rope(0, 0)
            convolve(0, slice(B // 2, B), conv_done0, DC)
            rope(0, 1)
            convolve(1, slice(B // 2, B), conv_done2)
            negmax(0, 0)
            for e in range(EB):
                for h in range(2):
                    dve.wait_ge(dt_ps, 2 * e + h + 1)
                    nc.vector.tensor_scalar(delta[:, e, h * 512:(h + 1) * 512], ps_r[:, h, :],
                                            par[:, e, DC + 1:DC + 2], None, ALU.add).then_inc(dt_v, 1)
            reciprocals(0, 0)

            def prepare_scan(g):
                if g == 1:
                    dve.wait_ge(a_done, 1)
                    nc.vector.tensor_scalar(a_neg[:], a_exp[:], -1.0, None, ALU.mult).then_inc(ssm_ready, 1)
                    for e in range(EB):
                        dve.wait_ge(sp_e, 2 * (e + 1))
                        nc.vector.tensor_scalar(state[:, e, :], decay[:, e, :], 1.0, None, ALU.add
                                                ).then_inc(sp_w, 1)
                    for e in range(EB):
                        dve.wait_ge(sp_w, e + 1)
                        nc.vector.scalar_tensor_tensor(decay[:, e, :], state[:, e, :], 1.0, decay[:, e, :],
                                                       ALU.subtract, ALU.subtract).then_inc(sp_c, 1)
                if g >= 2:
                    e = g - 2
                    dve.wait_ge(sp_c, e + 1)
                    dve.wait_ge(sp_l, e + 1)
                    then(nc.vector.tensor_tensor(y[:, e, :], y[:, e, :], decay[:, e, :], ALU.subtract))
                    then(nc.vector.scalar_tensor_tensor(delta[:, e, :], delta[:, e, :], 0.0, y[:, e, :],
                                                        ALU.max, ALU.add))
                    dve.wait_ge(u_done, e + 1)
                    nc.vector.tensor_tensor(du[:, e, :], delta[:, e, :], u_s[:, e, :], ALU.mult
                                            ).then_inc(ssm_ready, 1)
                    nc.vector.tensor_scalar(y[:, e, :], u_s[:, e, :], par[:, e, DC + 2:DC + 3], None, ALU.mult
                                            ).then_inc(ssm_ready, 1)
                    nc.vector.memset(decay[:, e, :].rearrange("p (b s) -> p b s", b=B)[:, :, 0:1], 0.0
                                     ).then_inc(decay_free, 1)

            def drive(b, g):
                u = mulof(b, KVH) + g
                n = b * (KVH // 2) + g // 2
                r = (g // 2) % 2
                dve.wait_ge(bc_in[r], (b * 2 + g // 4 + 1) * 32)
                dve.wait_ge(state_free, u + 1)
                nc.vector.tensor_tensor(state[:, g % 2, :], du[:, g % 2, :], bc[:, r, 0, :], ALU.mult
                                        ).then_inc(drive_done, 1)

            def scan(b, g):
                u = mulof(b, KVH) + g
                dve.wait_ge(drive_done, u + 1)
                dve.wait_ge(decay_done, u + 1)
                nc.vector.tensor_tensor_scan(state[:, g % 2, :], decay[:, g % 2, :], state[:, g % 2, :], 0.0,
                                             ALU.mult, ALU.add).then_inc(decay_free, 1)

            def times_c(b, g):
                u = mulof(b, KVH) + g
                dve.wait_ge(decay_free, u + 3)
                nc.vector.tensor_tensor(state[:, g % 2, :], state[:, g % 2, :],
                                        bc[:, (g // 2) % 2, 1, :], ALU.mult).then_inc(hc_done, 1)

            def copy_pt(b, g):
                u = mulof(b, KVH) + g
                dve.wait_ge(pt_done, u * 3 + 2)
                nc.vector.tensor_copy(pt[:, 1, :], ps_r[:, (5 * g + 1) % 2, :]).then_inc(pt_1, 1)

            def next_x(b):
                dve.wait_ge(proj_done, b * 16 + 16)
                nc.vector.tensor_copy(xt[:], xt_all[:, :, bass.ds((b + 1) * S, S)]).then_inc(xt_ready, 1)

            def add_attention(b):
                dve.wait_ge(wo_done, b + 2)
                o = ps_p[:, :, 0:HID] if isinstance(b, int) and b == LAST else ps_o[:].rearrange(
                    "p (t n) -> p t n", t=TB)
                nc.vector.tensor_tensor(x1[:, bass.ds(b * TB, TB), :], o,
                                        xs[:, bass.ds(b * TB, TB), :], ALU.add).then_inc(x1_done, 1)

            def dequantise_gate():
                dve.wait_ge(ffn_in, 16 * 8)
                nc.vector.tensor_scalar(wgu[:, 0, :, :], wgu_i[:], ZERO_POINT, None, ALU.subtract
                                        ).then_inc(wq_done, 1)

            def dequantise_up_down():
                dve.wait_ge(up_in, 16)
                nc.vector.tensor_scalar(wgu[:, 1, :, :], wgu_i[:], ZERO_POINT, None, ALU.subtract
                                        ).then_inc(wq_done, 1)
                for i in range(HT):
                    m = HP[i]
                    nc.vector.scalar_tensor_tensor(wdn[0:m, i, :], wdn_i[0:m, i, :], ZERO_POINT,
                                                   sdn[0:m, :], ALU.subtract, ALU.mult).then_inc(wq_done, 1)

            def x1_stats(lo, hi):
                dve.wait_ge(x1_done, 1 + hi)
                for i in range(lo * TB, hi * TB):
                    nc.vector.bn_stats(stats[:, i, :], x1[:, i, :]).then_inc(v_chain, 1)
                chain[0] += (hi - lo) * TB
                dve.wait_ge(v_chain, chain[0])
                for i in range(lo * TB, hi * TB):
                    nc.vector.bn_aggr(mv1[:, i, :], stats[:, i, :]).then_inc(st1_done, 1)

            def x1_nmr(lo, hi, step):
                dve.wait_ge(r1_done, step)
                nc.vector.scalar_tensor_tensor(nmr1[:, lo * TB:hi * TB], mv1[:, lo * TB:hi * TB, 0], -1.0,
                                               rstd1[:, lo * TB:hi * TB], ALU.mult, ALU.mult
                                               ).then_inc(r1_done, 1)

            def batch(b, first, last):
                for g in range(KVH):
                    if not (last and g + 2 >= KVH):
                        rope(b, g + 2)
                    if not (last and g + 1 >= KVH):
                        negmax(b, g + 1)
                    if g == 0 and not first:
                        add_attention(b - 1)
                    if not last:
                        copy_pt(b, g)
                    units = scans(b, g)
                    if units:
                        drive(*units[0])
                        scan(*units[0])
                    if not (last and g + 1 >= KVH):
                        reciprocals(b, g + 1)
                    if units:
                        times_c(*units[0])
                    for v in units[1:]:
                        drive(*v)
                        scan(*v)
                        times_c(*v)
                    if first and g < 4:
                        prepare_scan(g)
                    if g == 4 and not last:
                        next_x(b)
                    if last and g == 1:
                        x1_stats(0, LAST)
                    if last and g == 3:
                        x1_nmr(0, LAST, 1)
                    if first and g == KVH - 3:
                        dequantise_gate()
                    if last and g == 2:
                        dequantise_up_down()

            dve.wait_ge(xt_sb, B)
            batch(0, True, False)
            with dve.Fori(1, LAST) as b:
                batch(b, False, False)
            batch(LAST, False, True)

            dve.wait_ge(state_free, UNITS + 2)

            def gate_z(b):
                dve.wait_ge(sz_done, b * TB + TB)
                if not (isinstance(b, int) and b == 0):
                    dve.wait_ge(gt_ps, b)
                nc.vector.tensor_tensor(gz, y[:, :, bass.ds(b * S, S)], sz, ALU.mult).then_inc(gz_done, 1)

            def sum_x2(b):
                dve.wait_ge(gt_ps, b + 1)
                nc.vector.tensor_tensor(xs[:, bass.ds(b * TB, TB), :],
                                        ps_r[:, 0, :].rearrange("p (t n) -> p t n", t=TB),
                                        x1[:, bass.ds(b * TB, TB), :], ALU.add).then_inc(x2_done, 1)
                dve.wait_ge(x1_done, 2)
                dve.wait_ge(x2_done, b + 1)
                for t in range(TB):
                    nc.vector.bn_stats(stats[:, t, :], xs[:, bass.ds(b * TB + t, 1), :].rearrange(
                        "p a n -> p (a n)")).then_inc(bn2_done, 1)
                dve.wait_ge(x1_done, 2)
                dve.wait_ge(bn2_done, b * TB + TB)
                for t in range(TB):
                    nc.vector.bn_aggr(mv2[:, t, :], stats[:, t, :]).then_inc(st2_done, 1)

            def norm_x2(b):
                dve.wait_ge(r2_done, b + 1)
                dve.wait_ge(st2_done, b * TB + TB)
                for t in range(TB):
                    nc.vector.tensor_scalar(xh2[:, t, :], xs[:, bass.ds(b * TB + t, 1), :], mv2[:, t, 0:1],
                                            rstd2[:, t:t + 1], ALU.subtract, ALU.mult).then_inc(xh2_done, 1)

            def split_x2(b):
                dve.wait_ge(x2t_sb, b + 1)
                nc.vector.tensor_tensor(xh2_t[:, 1, :, :], ps_r[:, 1, :].rearrange("p (k s) -> p k s", k=KT),
                                        xh2_t[:, 0, :, :], ALU.subtract).then_inc(x2lo_done, 1)

            def hidden(b, i):
                m = HP[i]
                dve.wait_ge(gate_done, b * HT + i + 1)
                if i == 0 and not (isinstance(b, int) and b == 0):
                    dve.wait_ge(dn_ps, b * TB)
                nc.vector.scalar_tensor_tensor(hid_t[0:m, i, :], ps_s[0:m, i % 3, S:2 * S],
                                               sgu[0:m, 1, i:i + 1], gate[0:m, i % 2, :],
                                               ALU.mult, ALU.mult).then_inc(hid_done, 1)

            def result(b):
                dve.wait_ge(dn_ps, b * TB + TB)
                nc.vector.tensor_tensor(x1[:, bass.ds(b * TB, TB), :], ps_p[:, :, 0:HID],
                                        xs[:, bass.ds(b * TB, TB), :], ALU.add).then_inc(res_done, 1)

            def ffn(b, last):
                if not last:
                    gate_z(b + 1)
                for i in range(HT):
                    hidden(b, i)
                    if i == 0 and not last:
                        sum_x2(b + 1)
                    if i == 3 and not last:
                        norm_x2(b + 1)
                if not last:
                    split_x2(b + 1)
                if isinstance(b, int) and b == 0:
                    x1_stats(LAST, B)
                    x1_nmr(LAST, B, 3)
                result(b)

            gate_z(0)
            sum_x2(0)
            add_attention(LAST)
            norm_x2(0)
            split_x2(0)
            ffn(0, False)
            with dve.Fori(1, LAST) as b:
                ffn(b, False)
            ffn(LAST, True)

        @block.tensor
        def _(pe):
            pe.sem_inc(wo_done, 1)
            pe.wait_ge(consts, 9)

            def transpose_x(i):
                pe.wait_ge(ln_x, TB * (i + 1))
                if i >= 2:
                    pe.wait_ge(xt_sb, i - 1)
                for k in range(KT):
                    for t in range(TB):
                        last = nc.tensor.transpose(ps_r[:, i % 2, k * S + t * P:k * S + (t + 1) * P],
                                                   x1[:, i * TB + t, k * P:(k + 1) * P], ident[:])
                last.then_inc(xt_ps, 1)

            pe.wait_ge(ctx_in, 32)
            for i in range(2 * EB):
                e, h = divmod(i, 2)
                dst = ps_s[:, i, :] if i < 3 else ps_o[:]
                nc.tensor.matmul(dst, inproj[:, e * P:(e + 1) * P], ctxs[:, h * 512:(h + 1) * 512],
                                 start=True, stop=True).then_inc(inp_ps, 1)
            for i in range(B):
                transpose_x(i)

            def project(b, g, blocks=range(TB)):
                u = mulof(b, KVH) + g
                gg = g % KVH
                if gg == 0 and 0 in blocks:
                    pe.wait_ge(xt_ready, b + 1 + g // KVH)
                for t in blocks:
                    if not (isinstance(b, int) and 8 * b + g < 1):
                        pe.wait_ge(rope_mul, u * 4 - 2 * (TB - 1 - t))
                        pe.wait_ge(v_copied, u * 2 - (TB - 1 - t))
                    for k in range(KT):
                        last = nc.tensor.matmul(ps_p[:, t, 0:GC], xt[:, k, t * P:(t + 1) * P],
                                                wqkv[:, k, gg, :], start=(k == 0), stop=(k == KT - 1))
                    last.then_inc(proj_done, 1)

            def transpose_qk(b, g):
                u = mulof(b, KVH) + g
                slot = g - 2
                for t in range(TB):
                    pe.wait_ge(rope_add, u * 4 + 2 * (t + 1))
                    bank = (5 * slot + 3 + t) % 2
                    if t == 0:
                        if isinstance(b, int) and b == 0 and g == 0:
                            pe.wait_ge(xt_sb, B)
                        else:
                            pe.wait_ge(qkt_copied, u * 2)
                        if slot >= 0:
                            pe.wait_ge(pt_1, u)
                    elif slot >= 0:
                        pe.wait_ge(pt_act, u * 2 - 1)
                    for k in range(3):
                        last = nc.tensor.transpose(ps_r[:, bank, k * P:(k + 1) * P],
                                                   qkn[:, g % 2, t, k * P:(k + 1) * P], ident[:])
                    last.then_inc(qkt_done, 1)

            def scores(b, g):
                u = mulof(b, KVH) + g
                r = g % 2
                pe.wait_ge(qkt_copied, u * 2 + 2)
                first = isinstance(b, int) and 8 * b + g < 1

                def dot(bank, col, h, t, keys, start=False):
                    lo = (h % 2) * HD
                    return nc.tensor.matmul(ps_s[:, bank, col:col + keys],
                                            qkt[lo:lo + HD, r, h // 2, t * P:(t + 1) * P],
                                            qkt[lo:lo + HD, r, 2, 0:keys], start=start, stop=False)

                def mask(bank):
                    if bank == 0:
                        o, m = ps_s[:, 0, :], mask_diag[:]
                    else:
                        o = ps_s[:, bank, :].rearrange("p (h t k) -> p h t k", h=2, t=TB)[:, :, 1, :]
                        m = mask_diag[:, 0:2 * P].rearrange("p (h k) -> p h k", h=2)
                    nc.tensor.matmul(o, ident_b[:], m, start=False, stop=True).then_inc(score_done, 1)

                if first:
                    pe.wait_ge(inp_sb, 2 * EB)
                else:
                    pe.wait_ge(exp_done, u * 8)
                dot(0, 0, 0, 0, P, start=True)
                dot(2, 0, 1, 1, S, start=True)
                dot(0, 2 * P, 2, 0, P).then_inc(even_done, 1)
                dot(2, S, 3, 1, S)
                mask(2)
                dot(1, 0, 0, 1, S, start=True)
                pe.wait_ge(even_done, u + 1)
                dot(0, P, 1, 0, P)
                dot(1, S, 2, 1, S)
                mask(1)
                dot(0, 3 * P, 3, 0, P)
                mask(0)

            place = [0, 2, 1, 3]

            def transpose_p(b, g, qk_before, fills):
                u = mulof(b, KVH) + g
                r = g % 2
                if 0 in fills:
                    pe.wait_ge(norm_done, u * 8 + 9)
                for fill in fills:
                    bank = (5 * g + fill) % 2
                    if fill == 2:
                        pe.wait_ge(pt_act, u * 2 + 2)
                    elif qk_before:
                        pe.wait_ge(qkt_copied, u * 2 + 3 + fill)
                    elif fill == 0:
                        pe.wait_ge(pt_1, u + 1)
                    else:
                        pe.wait_ge(pt_act, u * 2 + 1)
                    for k in range(4):
                        if fill < 2:
                            h = 2 * fill + k // 2
                            src = prob0[:, r, h, :] if k % 2 == 0 else prob1[:, r, place[h], 0:P]
                        else:
                            src = prob1[:, r, place[k], P:S]
                        last = nc.tensor.transpose(ps_r[:, bank, k * P:(k + 1) * P], src, ident[:])
                    last.then_inc(pt_done, 1)

            def values(b, g):
                u = mulof(b, KVH) + g
                if not (isinstance(b, int) and 8 * b + g < 1):
                    pe.wait_ge(attn_copied, u + 1)
                    if g == 0:
                        pe.wait_ge(x1_done, b + 1)
                pe.wait_ge(v_copied, u * 2 + 2)
                pe.wait_ge(pt_act, u * 2 + 3)
                pe.wait_ge(pt_1, u + 2)
                for pair in range(GRP // 2):
                    for part in range(2):
                        for odd in range(2):
                            o = ps_o[odd * HD:(odd + 1) * HD, :]
                            if part == 0:
                                last = nc.tensor.matmul(o[:, pair * S:(pair + 1) * S], vv[:, g % 4, 0, :],
                                                        pt[:, pair, odd * S:(odd + 1) * S], start=True, stop=False)
                            else:
                                h = 2 * pair + odd
                                last = nc.tensor.matmul(o[:, pair * S + P:(pair + 1) * S], vv[:, g % 4, 1, :],
                                                        pt[:, 2, h * P:(h + 1) * P], start=False, stop=True)
                last.then_inc(pv_done, 1)

            def out_project(b, t, units=range(KVH)):
                last_b = isinstance(b, int) and b == LAST
                o = ps_p[:, t, 0:HID] if last_b else ps_o[:, t * HID:(t + 1) * HID]
                pe.wait_ge(wo_in, 16)
                pe.wait_ge(attn_copied, b * 8 + units[-1] + 2)
                ks = range(2 * units[0], 2 * units[-1] + 2)
                for k in ks:
                    last = nc.tensor.matmul(o, attn_t[:, k, t * P:(t + 1) * P], wo[:, k, :],
                                            start=(k == 0), stop=(k == H // 2 - 1))
                if t == TB - 1 and units[-1] == KVH - 1:
                    last.then_inc(wo_done, 1)

            pe.wait_ge(wqkv_in, 16)
            project(0, 0)
            project(0, 1)
            transpose_qk(0, 0)
            transpose_qk(0, 1)
            scores(0, 0)
            pe.wait_ge(ssm_in, 32)
            pe.wait_ge(u_done, EB)
            pe.wait_ge(rope_mul, 8)
            pe.wait_ge(v_copied, 4)
            for h in range(2):
                for e in range(EB):
                    last = nc.tensor.matmul(ps_p[0:XR, h, :], xproj[:, e, :], u_s[:, e, h * 512:(h + 1) * 512],
                                            start=(e == 0), stop=(e == EB - 1))
                last.then_inc(xdbl_ps, 1)
            pe.wait_ge(xdbl_sb, 2)
            pe.wait_ge(qkt_copied, 4)
            for e in range(EB):
                for h in range(2):
                    if e == 1:
                        pe.wait_ge(dt_v, h + 1)
                    nc.tensor.matmul(ps_r[:, h, :], dtproj[:, e * P:(e + 1) * P], xdbl[0:DR, h * 512:(h + 1) * 512],
                                     start=True, stop=True).then_inc(dt_ps, 1)
            pe.wait_ge(wqkv_in2, 16)
            pe.wait_ge(dt_v, 2 * EB)
            project(0, 2)

            def batch(b, first, last):
                for g in range(KVH):
                    if not (last and g + 1 >= KVH):
                        scores(b, g + 1)
                    if g == 0 and not first:
                        for t in range(TB):
                            out_project(b - 1, t)
                    transpose_p(b, g, not (last and g + 1 >= KVH), [0, 1])
                    if not (last and g + 3 >= KVH):
                        project(b, g + 3, [0])
                    transpose_p(b, g, not (last and g + 1 >= KVH), [2])
                    if not (last and g + 3 >= KVH):
                        project(b, g + 3, [1])
                    if not (last and g + 2 >= KVH):
                        transpose_qk(b, g + 2)
                    values(b, g)
                    if last and g == KVH - 2:
                        pe.wait_ge(rope_mul, 4 * UNITS)
                        pe.wait_ge(v_copied, 2 * UNITS)
                        out_project(b, 0, range(KVH - 2))
                if last:
                    out_project(b, 0, range(KVH - 2, KVH))
                    out_project(b, 1, range(KVH - 2))
                    transpose_gz(0)
                    out_project(b, 1, range(KVH - 2, KVH))

            def transpose_gz(b):
                pe.wait_ge(gz_done, b + 1)
                if isinstance(b, int) and b == 0:
                    pe.wait_ge(pt_1, 1 + UNITS)
                    pe.wait_ge(pt_act, 1 + 2 * UNITS)
                else:
                    pe.wait_ge(x2_done, b)
                for lt in range(TB):
                    for et in range(EB):
                        last = nc.tensor.transpose(ps_r[:, 0, lt * HID + et * P:lt * HID + (et + 1) * P],
                                                   gz[:, et, lt * P:(lt + 1) * P], ident[:])
                last.then_inc(gt_ps, 1)

            def transpose_x2(b):
                pe.wait_ge(xh2_done, b * TB + TB)
                if not (isinstance(b, int) and b == 0):
                    pe.wait_ge(x2lo_done, b)
                for k in range(KT):
                    for t in range(TB):
                        last = nc.tensor.transpose(ps_r[:, 1, k * S + t * P:k * S + (t + 1) * P],
                                                   xh2[:, t, k * P:(k + 1) * P], ident[:])
                last.then_inc(x2t_ps, 1)

            def gate_up(b, tiles):
                pe.wait_ge(x2lo_done, b + 1)
                for i in tiles:
                    m = HP[i]
                    if not (isinstance(b, int) and b == 0 and i < 3):
                        pe.wait_ge(hid_done, b * HT + i - 2)
                    for w in range(2):
                        for k in range(KT):
                            for c in range(2):
                                last = nc.tensor.matmul(ps_s[0:m, i % 3, w * S:(w + 1) * S],
                                                        wgu[:, w, k, i * P:i * P + m], xh2_t[:, c, k, :],
                                                        start=(k == 0 and c == 0),
                                                        stop=(k == KT - 1 and c == 1))
                    last.then_inc(gu_ps, 1)

            def down(b):
                pe.wait_ge(hid_done, b * HT + HT)
                if isinstance(b, int) and b == 0:
                    pe.wait_ge(x1_done, 1 + B)
                if not (isinstance(b, int) and b == 0):
                    pe.wait_ge(res_done, b)
                for t in range(TB):
                    for i in range(HT):
                        m = HP[i]
                        last = nc.tensor.matmul(ps_p[:, t, 0:HID], hid_t[0:m, i, t * P:(t + 1) * P],
                                                wdn[0:m, i, :], start=(i == 0), stop=(i == HT - 1))
                    last.then_inc(dn_ps, 1)

            def ffn(b, last):
                gate_up(b, range(0, 1))
                if not last:
                    transpose_gz(b + 1)
                gate_up(b, range(1, HT))
                if not last:
                    transpose_x2(b + 1)
                down(b)

            batch(0, True, False)
            with pe.Fori(1, LAST) as b:
                batch(b, False, False)
            batch(LAST, False, True)

            pe.wait_ge(wq_done, 2 + HT)
            transpose_x2(0)
            ffn(0, False)
            with pe.Fori(1, LAST) as b:
                ffn(b, False)
            ffn(LAST, True)


def kernel(x, ctx_1024, L0_attn_Wq, L0_attn_Wk, L0_attn_Wv, L0_attn_Wo, L0_xattn_in_proj_w, L0_xattn_conv_w,
           L0_xattn_conv_b, L0_xattn_x_proj_w, L0_xattn_dt_proj_w, L0_xattn_dt_proj_b, L0_xattn_A_log,
           L0_xattn_D, L0_ffn_wq_gate, L0_ffn_s_gate, L0_ffn_wq_up, L0_ffn_s_up, L0_ffn_wq_down,
           L0_ffn_s_down):
    import concourse.bacc as bacc
    from concourse.bass_utils import run_bass_kernel_spmd

    inv = (1.0 / (10000.0 ** (np.arange(0, HD, 2, dtype=np.float32) / np.float32(HD)))).astype(np.float32)
    freq = np.arange(S, dtype=np.float32)[:, None] * inv[None, :]
    cos, sin = np.cos(freq), np.sin(freq)
    scale = np.repeat(np.array([HD ** -0.5] * GRP + [1.0], np.float32), HD)
    cos_t = (np.tile(cos, (1, 2 * (GRP + 1))) * scale).astype(np.float32)
    sin_t = (np.tile(np.concatenate([-sin, sin], 1), (1, GRP + 1)) * scale).astype(np.float32)

    rows = [np.asarray(w).reshape(KVH, -1, HID) for w in (L0_attn_Wq, L0_attn_Wk, L0_attn_Wv)]
    column = lambda v: np.asarray(v).reshape(DI, -1)
    arrays = {
        "x": np.asarray(x).reshape(L, HID),
        "ctx_t": np.asarray(ctx_1024).reshape(L, DM).T,
        "wqkv_t": np.concatenate(rows, 1).transpose(2, 0, 1),
        "wo_t": np.asarray(L0_attn_Wo).T,
        "cos_t": cos_t,
        "sin_t": sin_t,
        "inproj_t": np.asarray(L0_xattn_in_proj_w).T,
        "ssm_par": np.concatenate([column(v) for v in (L0_xattn_conv_w, L0_xattn_conv_b, L0_xattn_dt_proj_b,
                                                       L0_xattn_D, L0_xattn_A_log)], 1),
        "xproj_t": np.asarray(L0_xattn_x_proj_w).T,
        "dtproj_t": np.asarray(L0_xattn_dt_proj_w).T,
        "wgate_t": np.asarray(L0_ffn_wq_gate).T,
        "wup_t": np.asarray(L0_ffn_wq_up).T,
        "wdown_t": np.asarray(L0_ffn_wq_down).T,
        "s_gate": np.asarray(L0_ffn_s_gate),
        "s_up": np.asarray(L0_ffn_s_up),
        "s_down": np.asarray(L0_ffn_s_down),
    }
    arrays = {k: np.ascontiguousarray(v) for k, v in arrays.items()}
    nc = bacc.Bacc("TRN2", target_bir_lowering=False, num_devices=1)
    args = [nc.dram_tensor(k, v.shape, mybir.dt.from_np(v.dtype), kind="ExternalInput").ap()
            for k, v in arrays.items()]
    bc_scratch = nc.dram_tensor("bc_scratch", (2 * NS, L), F32, kind="Internal").ap()
    out = nc.dram_tensor("out", (B, S, HID), F32, kind="ExternalOutput").ap()
    decoder_layer(nc, *args, bc_scratch, out)
    r = run_bass_kernel_spmd(nc, [arrays], core_ids=[0])
    return r.results[0]["out"]
```
